# Optimizing a Trainium2 kernel written in Bass

```python
import numpy as np
import jax
import jax.numpy as jnp

def _softmax(x, axis=-1):
    return jax.nn.softmax(x, axis=axis)

def _gelu(x):
    return jax.nn.gelu(x, approximate=True)

def _silu(x):
    return jax.nn.silu(x)

def _sigmoid(x):
    return jax.nn.sigmoid(x)

def _layernorm(x, axis=-1, eps=1e-05):
    m = jnp.mean(x, axis=axis, keepdims=True)
    v = jnp.var(x, axis=axis, keepdims=True)
    return (x - m) / jnp.sqrt(v + eps)

def _scatter_add(tgt, idx, src, axis=0):
    return tgt.at[idx].add(src)

def _segment_sum(src, seg, n):
    return jax.ops.segment_sum(src, seg, n)
kernel_name = 'mk_adaln_d2_jaxref_r8_dd9658'

def setup_inputs(seed: int=0):
    np.random.seed(seed)
    _w = jnp.asarray

    def _L0_attn_setup():
        import jax, jax.numpy as jnp
        import numpy as np
        D_MODEL = 128
        N_HEADS = 16
        LATENT_HEADS = 8
        LATENT_DIM = 64
        N_LATENTS = 64
        WINDOW = 32
        HEAD_DIM = D_MODEL // N_HEADS
        LAT_HD = LATENT_DIM // LATENT_HEADS
        B, S = (2, 512)

        def _pool_to_latents(x):
            Bx, Sx, C = x.shape
            chunk = max(1, Sx // N_LATENTS)
            return x.reshape(Bx, N_LATENTS, chunk, C).mean(axis=2)

        def _local_window_attn(Q, K, V):
            Bx, H, Sx, D = Q.shape
            W = WINDOW
            nb = Sx // W
            Qb = Q.reshape(Bx, H, nb, W, D)
            Kp = jnp.pad(K, ((0, 0), (0, 0), (W, 0), (0, 0))).reshape(Bx, H, nb + 1, W, D)
            Vp = jnp.pad(V, ((0, 0), (0, 0), (W, 0), (0, 0))).reshape(Bx, H, nb + 1, W, D)
            Kw = jnp.concatenate([Kp[:, :, :-1], Kp[:, :, 1:]], axis=3)
            Vw = jnp.concatenate([Vp[:, :, :-1], Vp[:, :, 1:]], axis=3)
            i = jnp.arange(W)[:, None]
            j = jnp.arange(2 * W)[None, :]
            base = (j > i) & (j <= i + W)
            blk0 = (jnp.arange(nb) > 0)[:, None, None] | (j >= W)[None, :, :]
            mask = base[None, :, :] & blk0
            sc = jnp.einsum('bhnid,bhnjd->bhnij', Qb, Kw) / np.sqrt(D).astype(np.float32)
            sc = jnp.where(mask[None, None], sc, -jnp.inf)
            p = jax.nn.softmax(sc, axis=-1)
            out = jnp.einsum('bhnij,bhnjd->bhnid', p, Vw)
            return out.reshape(Bx, H, Sx, D)
        key = jax.random.key(seed)
        ks = jax.random.split(key, 11)
        std = 0.02
        w = lambda k, shp: jax.random.normal(k, shp, jnp.float32) * std
        return {'x': jax.random.normal(ks[0], (B, S, D_MODEL), jnp.float32), 'wq': w(ks[1], (D_MODEL, D_MODEL)), 'wk': w(ks[2], (D_MODEL, D_MODEL)), 'wv': w(ks[3], (D_MODEL, D_MODEL)), 'wgq': w(ks[4], (D_MODEL, LATENT_DIM)), 'wgk': w(ks[5], (D_MODEL, LATENT_DIM)), 'wgv': w(ks[6], (D_MODEL, LATENT_DIM)), 'r_out_w': w(ks[7], (LATENT_DIM, D_MODEL)), 'gate_local_w': w(ks[8], (N_HEADS, HEAD_DIM)), 'gate_remote_w': w(ks[9], (N_HEADS, HEAD_DIM)), 'w_out': w(ks[10], (D_MODEL, D_MODEL))}
    _L0_attn_in = _L0_attn_setup()

    def _L0_ffn_setup():
        import jax, jax.numpy as jnp
        import numpy as np
        B, S, F, E, K = (4, 128, 128, 8, 2)
        H = 4 * F
        key = jax.random.key(seed)
        ks = jax.random.split(key, 7)

        def xavier(k, shape):
            fan_in, fan_out = (shape[-2], shape[-1])
            scale = jnp.sqrt(6.0 / (fan_in + fan_out))
            return jax.random.uniform(k, shape, jnp.float32, -scale, scale)
        return {'x': jax.random.normal(ks[0], (B, S, F), jnp.float32), 'Wg': xavier(ks[1], (F, E)), 'bg': jnp.zeros((E,), jnp.float32), 'W1': xavier(ks[2], (E, F, H)), 'b1': jnp.zeros((E, H), jnp.float32), 'W2': xavier(ks[3], (E, H, F)), 'b2': jnp.zeros((E, F), jnp.float32)}
    _L0_ffn_in = _L0_ffn_setup()
    _L0_c = _w((lambda *s: np.random.randn(*s).astype(np.float32) * 0.05)(8, 128))
    _L0_wmod = _w((lambda *s: np.random.randn(*s).astype(np.float32) * 0.05)(128, 6 * 128) * 128 ** (-0.5))

    def _L1_attn_setup():
        import jax, jax.numpy as jnp
        import numpy as np
        WINDOW = 64

        def _block_local_attn(q, k, v, window):
            B, H, T, D = q.shape
            W = window
            nb = T // W
            scale = 1.0 / jnp.sqrt(jnp.asarray(D, q.dtype))
            qb = q.reshape(B, H, nb, W, D)
            kb = k.reshape(B, H, nb, W, D)
            vb = v.reshape(B, H, nb, W, D)
            kp = jnp.pad(kb, ((0, 0), (0, 0), (1, 0), (0, 0), (0, 0)))[:, :, :nb]
            vp = jnp.pad(vb, ((0, 0), (0, 0), (1, 0), (0, 0), (0, 0)))[:, :, :nb]
            k2 = jnp.concatenate([kp, kb], axis=3)
            v2 = jnp.concatenate([vp, vb], axis=3)
            i = jnp.arange(W)[:, None]
            j = jnp.arange(2 * W)[None, :]
            base = (j > i) & (j <= i + W)
            prev_ok = (jnp.arange(nb)[:, None] > 0) | (jnp.arange(2 * W)[None, :] >= W)
            mask = base[None, :, :] & prev_ok[:, None, :]
            scores = jnp.einsum('bhnqd,bhnkd->bhnqk', qb, k2) * scale
            scores = jnp.where(mask[None, None], scores, jnp.asarray(-1e+30, scores.dtype))
            p = jax.nn.softmax(scores, axis=-1)
            out = jnp.einsum('bhnqk,bhnkd->bhnqd', p, v2)
            return out.reshape(B, H, T, D)
        key = jax.random.key(seed)
        ks = jax.random.split(key, 5)
        B, T, C = (2, 1024, 128)
        s = 1.0 / np.sqrt(C)
        return {'x': jax.random.normal(ks[0], (B, T, C), dtype=jnp.float32), 'Wq': jax.random.normal(ks[1], (C, C), dtype=jnp.float32) * s, 'Wk': jax.random.normal(ks[2], (C, C), dtype=jnp.float32) * s, 'Wv': jax.random.normal(ks[3], (C, C), dtype=jnp.float32) * s, 'Wo': jax.random.normal(ks[4], (C, C), dtype=jnp.float32) * s}
    _L1_attn_in = _L1_attn_setup()

    def _L1_ffn_setup():
        import jax, jax.numpy as jnp
        import numpy as np
        BLOCK = 16
        _GRID = jnp.array([0.0, 0.5, 1.0, 1.5, 2.0, 3.0, 4.0, 6.0], dtype=jnp.float32)
        _MID = jnp.array([0.25, 0.75, 1.25, 1.75, 2.5, 3.5, 5.0], dtype=jnp.float32)

        def fp4_quant_dequant(x):
            shape = x.shape
            xb = x.reshape(shape[:-1] + (shape[-1] // BLOCK, BLOCK))
            scale = jnp.max(jnp.abs(xb), axis=-1, keepdims=True) / 6.0
            scale = jnp.maximum(scale, jnp.float32(1e-12))
            xn = xb / scale
            idx = jnp.searchsorted(_MID, jnp.abs(xn))
            q = _GRID[idx] * jnp.sign(xn) * scale
            return q.reshape(shape)

        def fp4_linear(x, w):
            xq = fp4_quant_dequant(x)
            wq = fp4_quant_dequant(w)
            return jnp.einsum('bsk,nk->bsn', xq, wq)
        key = jax.random.key(seed)
        k1, k2, k3, k4 = jax.random.split(key, 4)
        H, I = (128, 352)
        x = jax.random.normal(k1, (4, 512, H), dtype=jnp.float32)
        w_gate = jax.random.normal(k2, (I, H), dtype=jnp.float32) * 0.02
        w_up = jax.random.normal(k3, (I, H), dtype=jnp.float32) * 0.02
        w_down = jax.random.normal(k4, (H, I), dtype=jnp.float32) * 0.02
        return {'x': x, 'w_gate': w_gate, 'w_up': w_up, 'w_down': w_down}
    _L1_ffn_in = _L1_ffn_setup()
    _L1_c = _w((lambda *s: np.random.randn(*s).astype(np.float32) * 0.05)(8, 128))
    _L1_wmod = _w((lambda *s: np.random.randn(*s).astype(np.float32) * 0.05)(128, 6 * 128) * 128 ** (-0.5))
    _d = {'L0_attn_x': _L0_attn_in['x'], 'L0_attn_wq': _L0_attn_in['wq'], 'L0_attn_wk': _L0_attn_in['wk'], 'L0_attn_wv': _L0_attn_in['wv'], 'L0_attn_wgq': _L0_attn_in['wgq'], 'L0_attn_wgk': _L0_attn_in['wgk'], 'L0_attn_wgv': _L0_attn_in['wgv'], 'L0_attn_r_out_w': _L0_attn_in['r_out_w'], 'L0_attn_gate_local_w': _L0_attn_in['gate_local_w'], 'L0_attn_gate_remote_w': _L0_attn_in['gate_remote_w'], 'L0_attn_w_out': _L0_attn_in['w_out'], 'L0_ffn_Wg': _L0_ffn_in['Wg'], 'L0_ffn_bg': _L0_ffn_in['bg'], 'L0_ffn_W1': _L0_ffn_in['W1'], 'L0_ffn_b1': _L0_ffn_in['b1'], 'L0_ffn_W2': _L0_ffn_in['W2'], 'L0_ffn_b2': _L0_ffn_in['b2'], 'L0_c': _L0_c, 'L0_wmod': _L0_wmod, 'L1_attn_Wq': _L1_attn_in['Wq'], 'L1_attn_Wk': _L1_attn_in['Wk'], 'L1_attn_Wv': _L1_attn_in['Wv'], 'L1_attn_Wo': _L1_attn_in['Wo'], 'L1_ffn_w_gate': _L1_ffn_in['w_gate'], 'L1_ffn_w_up': _L1_ffn_in['w_up'], 'L1_ffn_w_down': _L1_ffn_in['w_down'], 'L1_c': _L1_c, 'L1_wmod': _L1_wmod}
    _x0 = _d['L0_attn_x']
    _d['L0_attn_x'] = jax.random.normal(jax.random.fold_in(jax.random.key(seed), 1), (8, 256, 128), dtype=_x0.dtype)
    del _x0
    return _d

def reference(L0_attn_x, L0_attn_wq, L0_attn_wk, L0_attn_wv, L0_attn_wgq, L0_attn_wgk, L0_attn_wgv, L0_attn_r_out_w, L0_attn_gate_local_w, L0_attn_gate_remote_w, L0_attn_w_out, L0_ffn_Wg, L0_ffn_bg, L0_ffn_W1, L0_ffn_b1, L0_ffn_W2, L0_ffn_b2, L0_c, L0_wmod, L1_attn_Wq, L1_attn_Wk, L1_attn_Wv, L1_attn_Wo, L1_ffn_w_gate, L1_ffn_w_up, L1_ffn_w_down, L1_c, L1_wmod):

    def _L0_attn_ref(x, wq, wk, wv, wgq, wgk, wgv, r_out_w, gate_local_w, gate_remote_w, w_out):
        import jax, jax.numpy as jnp
        import numpy as np
        D_MODEL = 128
        N_HEADS = 16
        LATENT_HEADS = 8
        LATENT_DIM = 64
        N_LATENTS = 64
        WINDOW = 32
        HEAD_DIM = D_MODEL // N_HEADS
        LAT_HD = LATENT_DIM // LATENT_HEADS
        B, S = (2, 512)

        def _pool_to_latents(x):
            Bx, Sx, C = x.shape
            chunk = max(1, Sx // N_LATENTS)
            return x.reshape(Bx, N_LATENTS, chunk, C).mean(axis=2)

        def _local_window_attn(Q, K, V):
            Bx, H, Sx, D = Q.shape
            W = WINDOW
            nb = Sx // W
            Qb = Q.reshape(Bx, H, nb, W, D)
            Kp = jnp.pad(K, ((0, 0), (0, 0), (W, 0), (0, 0))).reshape(Bx, H, nb + 1, W, D)
            Vp = jnp.pad(V, ((0, 0), (0, 0), (W, 0), (0, 0))).reshape(Bx, H, nb + 1, W, D)
            Kw = jnp.concatenate([Kp[:, :, :-1], Kp[:, :, 1:]], axis=3)
            Vw = jnp.concatenate([Vp[:, :, :-1], Vp[:, :, 1:]], axis=3)
            i = jnp.arange(W)[:, None]
            j = jnp.arange(2 * W)[None, :]
            base = (j > i) & (j <= i + W)
            blk0 = (jnp.arange(nb) > 0)[:, None, None] | (j >= W)[None, :, :]
            mask = base[None, :, :] & blk0
            sc = jnp.einsum('bhnid,bhnjd->bhnij', Qb, Kw) / np.sqrt(D).astype(np.float32)
            sc = jnp.where(mask[None, None], sc, -jnp.inf)
            p = jax.nn.softmax(sc, axis=-1)
            out = jnp.einsum('bhnij,bhnjd->bhnid', p, Vw)
            return out.reshape(Bx, H, Sx, D)
        Bx, Sx, _ = x.shape
        chunk = max(1, Sx // N_LATENTS)
        Q = (x @ wq).reshape(Bx, Sx, N_HEADS, HEAD_DIM).transpose(0, 2, 1, 3)
        K = (x @ wk).reshape(Bx, Sx, N_HEADS, HEAD_DIM).transpose(0, 2, 1, 3)
        V = (x @ wv).reshape(Bx, Sx, N_HEADS, HEAD_DIM).transpose(0, 2, 1, 3)
        local = _local_window_attn(Q, K, V)
        GQ = (x @ wgq).reshape(Bx, Sx, LATENT_HEADS, LAT_HD).transpose(0, 2, 1, 3)
        GK = _pool_to_latents(x @ wgk).reshape(Bx, N_LATENTS, LATENT_HEADS, LAT_HD).transpose(0, 2, 1, 3)
        GV = _pool_to_latents(x @ wgv).reshape(Bx, N_LATENTS, LATENT_HEADS, LAT_HD).transpose(0, 2, 1, 3)
        lsc = jnp.einsum('bhsd,bhnd->bhsn', GQ, GK) / np.sqrt(LAT_HD).astype(np.float32)
        lmask = jnp.arange(N_LATENTS)[None, :] <= (jnp.arange(Sx) // chunk)[:, None]
        lsc = jnp.where(lmask[None, None], lsc, -jnp.inf)
        lp = jax.nn.softmax(lsc, axis=-1)
        rem = jnp.einsum('bhsn,bhnd->bhsd', lp, GV)
        rem = rem.transpose(0, 2, 1, 3).reshape(Bx, Sx, LATENT_DIM) @ r_out_w
        rem = rem.reshape(Bx, Sx, N_HEADS, HEAD_DIM).transpose(0, 2, 1, 3)
        gl = jax.nn.sigmoid(jnp.einsum('bhsd,hd->bhs', Q, gate_local_w))[..., None]
        gr = jax.nn.sigmoid(jnp.einsum('bhsd,hd->bhs', Q, gate_remote_w))[..., None]
        out = gl * local + gr * rem
        out = out.transpose(0, 2, 1, 3).reshape(Bx, Sx, D_MODEL)
        return out @ w_out

    def _L0_ffn_ref(x, Wg, bg, W1, b1, W2, b2):
        import jax, jax.numpy as jnp
        import numpy as np
        B, S, F, E, K = (4, 128, 128, 8, 2)
        H = 4 * F
        gate_probs = jax.nn.softmax(x @ Wg + bg, axis=-1)
        k = K
        _, top_idx = jax.lax.top_k(gate_probs, k)
        expert_mask = jax.nn.one_hot(top_idx, gate_probs.shape[-1], dtype=gate_probs.dtype).sum(-2)
        selected = gate_probs * expert_mask
        selected = selected / (selected.sum(-1, keepdims=True) + 1e-08)
        h = jax.nn.gelu(jnp.einsum('bsf,efh->bseh', x, W1) + b1)
        expert_out = jnp.einsum('bseh,ehf->bsef', h, W2) + b2[None, None]
        return jnp.einsum('bsef,bse->bsf', expert_out, selected)

    def _L1_attn_ref(x, Wq, Wk, Wv, Wo):
        import jax, jax.numpy as jnp
        import numpy as np
        WINDOW = 64

        def _block_local_attn(q, k, v, window):
            B, H, T, D = q.shape
            W = window
            nb = T // W
            scale = 1.0 / jnp.sqrt(jnp.asarray(D, q.dtype))
            qb = q.reshape(B, H, nb, W, D)
            kb = k.reshape(B, H, nb, W, D)
            vb = v.reshape(B, H, nb, W, D)
            kp = jnp.pad(kb, ((0, 0), (0, 0), (1, 0), (0, 0), (0, 0)))[:, :, :nb]
            vp = jnp.pad(vb, ((0, 0), (0, 0), (1, 0), (0, 0), (0, 0)))[:, :, :nb]
            k2 = jnp.concatenate([kp, kb], axis=3)
            v2 = jnp.concatenate([vp, vb], axis=3)
            i = jnp.arange(W)[:, None]
            j = jnp.arange(2 * W)[None, :]
            base = (j > i) & (j <= i + W)
            prev_ok = (jnp.arange(nb)[:, None] > 0) | (jnp.arange(2 * W)[None, :] >= W)
            mask = base[None, :, :] & prev_ok[:, None, :]
            scores = jnp.einsum('bhnqd,bhnkd->bhnqk', qb, k2) * scale
            scores = jnp.where(mask[None, None], scores, jnp.asarray(-1e+30, scores.dtype))
            p = jax.nn.softmax(scores, axis=-1)
            out = jnp.einsum('bhnqk,bhnkd->bhnqd', p, v2)
            return out.reshape(B, H, T, D)
        B, T, C = x.shape
        H = 16
        D = C // H
        q = (x @ Wq.T).reshape(B, T, H, D).transpose(0, 2, 1, 3)
        k = (x @ Wk.T).reshape(B, T, H, D).transpose(0, 2, 1, 3)
        v = (x @ Wv.T).reshape(B, T, H, D).transpose(0, 2, 1, 3)
        out = _block_local_attn(q, k, v, WINDOW)
        out = out.transpose(0, 2, 1, 3).reshape(B, T, C)
        return out @ Wo.T

    def _L1_ffn_ref(x, w_gate, w_up, w_down):
        import jax, jax.numpy as jnp
        import numpy as np
        BLOCK = 16
        _GRID = jnp.array([0.0, 0.5, 1.0, 1.5, 2.0, 3.0, 4.0, 6.0], dtype=jnp.float32)
        _MID = jnp.array([0.25, 0.75, 1.25, 1.75, 2.5, 3.5, 5.0], dtype=jnp.float32)

        def fp4_quant_dequant(x):
            shape = x.shape
            xb = x.reshape(shape[:-1] + (shape[-1] // BLOCK, BLOCK))
            scale = jnp.max(jnp.abs(xb), axis=-1, keepdims=True) / 6.0
            scale = jnp.maximum(scale, jnp.float32(1e-12))
            xn = xb / scale
            idx = jnp.searchsorted(_MID, jnp.abs(xn))
            q = _GRID[idx] * jnp.sign(xn) * scale
            return q.reshape(shape)

        def fp4_linear(x, w):
            xq = fp4_quant_dequant(x)
            wq = fp4_quant_dequant(w)
            return jnp.einsum('bsk,nk->bsn', xq, wq)
        gate = fp4_linear(x, w_gate)
        y = fp4_linear(x, w_up)
        h = jax.nn.silu(gate) * y
        return fp4_linear(h, w_down)
    x = L0_attn_x
    mod = (_silu(L0_c) @ L0_wmod).reshape(L0_c.shape[0], 6, 1, -1)
    sa, ca, ga, sb, cb, gb = (mod[:, 0], mod[:, 1], mod[:, 2], mod[:, 3], mod[:, 4], mod[:, 5])
    ga = (2 * (ga >= 0) - 1) * jnp.maximum(jnp.abs(ga), 0.25)
    gb = (2 * (gb >= 0) - 1) * jnp.maximum(jnp.abs(gb), 0.25)
    h = _layernorm(x, axis=-1) * (1 + ca) + sa
    x = x + ga * _L0_attn_ref(h, L0_attn_wq, L0_attn_wk, L0_attn_wv, L0_attn_wgq, L0_attn_wgk, L0_attn_wgv, L0_attn_r_out_w, L0_attn_gate_local_w, L0_attn_gate_remote_w, L0_attn_w_out)
    h = _layernorm(x, axis=-1) * (1 + cb) + sb
    x = x + gb * _L0_ffn_ref(h, L0_ffn_Wg, L0_ffn_bg, L0_ffn_W1, L0_ffn_b1, L0_ffn_W2, L0_ffn_b2)
    mod = (_silu(L1_c) @ L1_wmod).reshape(L1_c.shape[0], 6, 1, -1)
    sa, ca, ga, sb, cb, gb = (mod[:, 0], mod[:, 1], mod[:, 2], mod[:, 3], mod[:, 4], mod[:, 5])
    ga = (2 * (ga >= 0) - 1) * jnp.maximum(jnp.abs(ga), 0.25)
    gb = (2 * (gb >= 0) - 1) * jnp.maximum(jnp.abs(gb), 0.25)
    h = _layernorm(x, axis=-1) * (1 + ca) + sa
    x = x + ga * _L1_attn_ref(h, L1_attn_Wq, L1_attn_Wk, L1_attn_Wv, L1_attn_Wo)
    h = _layernorm(x, axis=-1) * (1 + cb) + sb
    x = x + gb * _L1_ffn_ref(h, L1_ffn_w_gate, L1_ffn_w_up, L1_ffn_w_down)
    return x

_drawn_inputs = setup_inputs


def setup_inputs(seed=0):
    import zlib

    import numpy as np

    out = dict(_drawn_inputs(seed))
    spreads = {'L0_ffn_bg': (0.0, 0.544), 'L0_ffn_b1': (0.0, 0.526), 'L0_ffn_b2': (0.0, 0.424)}
    factors = {'L0_attn_wq': 8.0,
     'L0_attn_wk': 8.0,
     'L0_attn_wv': 8.0,
     'L0_attn_wgq': 8.0,
     'L0_attn_wgk': 8.0,
     'L0_attn_wgv': 8.0,
     'L0_attn_r_out_w': 8.0,
     'L0_attn_gate_local_w': 8.0,
     'L0_attn_gate_remote_w': 8.0,
     'L0_attn_w_out': 8.0,
     'L1_ffn_w_gate': 8.0,
     'L1_ffn_w_up': 8.0,
     'L1_ffn_w_down': 8.0}
    for name, (base, spread) in spreads.items():
        noise = np.random.default_rng([zlib.crc32(name.encode()), seed]).standard_normal(out[name].shape)
        drawn = base * np.exp(spread * noise) if base else spread * noise
        out[name] = jnp.asarray(drawn.astype(out[name].dtype))
    for name, factor in factors.items():
        out[name] = (out[name] * factor).astype(out[name].dtype)
    return out
```

```python
from contextlib import ExitStack

import concourse.bass as bass
from concourse import mybir

ALU = mybir.AluOpType
ACT = mybir.ActivationFunctionType
BF16 = mybir.dt.bfloat16
F32 = mybir.dt.float32
I32 = mybir.dt.int32
AX = mybir.AxisListType.X

P = 128
C = 128
B = 8
T = 2
H = 16
HD = 8
LATH = 8
NLAT = 64
E = 8
HC = 4
FH = 352
FCH = [(0, 128), (128, 128), (256, 96)]
NEG = -1e30
PAD = 64
K_ID = 0
K_LOC0 = K_ID + 128
K_LAT = K_LOC0 + 2 * 64
K_LOC1 = K_LAT + 2 * 64
K_Q0 = K_LOC1 + 2 * 128
K_Q1 = K_Q0 + 128
K_S = K_Q1 + 256
K_GK = K_S + 4
K_H = K_GK + 8
K_TRI = K_H + 16
K_SEL = K_TRI + 64
K_END = K_SEL + 8 * 128


def wait(eng, sem, value):
    if isinstance(value, int) and value <= 0:
        return
    eng.wait_ge(sem, value)


def settle(eng):
    eng.nop(nofuse=True)


class Chain:

    def __init__(self, eng, sem, start=0):
        self.eng, self.sem, self.n, self.it, self.per = eng, sem, start, None, 0

    def __call__(self, ins):
        ins.then_inc(self.sem, 1)
        self.n += 1
        self.eng.wait_ge(self.sem, self.n if self.it is None else self.it * self.per + self.n)

    def enter(self, it, first, per):
        self.it, self.per, self.at = it, per, self.n
        self.n -= first * per

    def leave(self, first, trips):
        took = self.n + first * self.per - self.at
        assert took == self.per, (self.sem, took, self.per)
        self.n = self.at + trips * self.per
        self.it = None


def has(b, lo, hi):
    return not isinstance(b, int) or lo <= b < hi


def run(eng, slots, slot, prologue, chains=()):
    prologue()
    for par in range(2):
        for k in range(slots):
            slot(par, k, par)
    with eng.Fori(1, B // 2 - 1) as it:
        for c in chains:
            c.enter(it, 1, c.per_pair)
        for par in range(2):
            for k in range(slots):
                slot(2 * it + par, k, par)
    for c in chains:
        c.leave(1, B // 2 - 2)
    for b in range(B - 2, B + 1):
        for k in range(slots):
            slot(b, k, b % 2)


def setup(nc, io, m, loads):
    with ExitStack() as ctx:
        def sb(name, shape, dt=F32):
            return ctx.enter_context(nc.sbuf_tensor(name, shape, dt))

        def sem(name):
            return ctx.enter_context(nc.semaphore(name))

        c_sb = sb("c_sb", [B, 2, C])
        c_exp = sb("c_exp", [B, 2, C])
        c_sig = sb("c_sig", [B, 2, C])
        c_silu = sb("c_silu", [B, 2, C])
        cT = sb("cT", [P, 2, B])
        wmod = [sb(f"wmod{i}", [P, 6 * C]) for i in range(2)]
        mod8 = sb("mod8", [B, 2, 6 * C])
        gsgn = sb("gsgn", [B, 2, 2, C])
        gabs = sb("gabs", [B, 2, 2, C])
        wqT0 = sb("wqT0", [P, C])
        gcol = sb("gcol", [P, 2])
        G = sb("G", [P, 2, H])
        wraw = sb("wraw", [P, 4, C])
        b1row = sb("b1row", [E * HC, C])
        ps = [ctx.enter_context(nc.psum_tensor(f"su{i}", [P, 512], F32)) for i in range(8)]
        s_small, s_c, s_wm, s_w0, s_exp, s_pe, s_dve, s_act, s_chain, s_ev, s_pool = [
            sem(n) for n in ["ld_const", "ld_c", "ld_wmod", "ld_w", "c_exp_done", "pe_filled", "dve_done",
                             "act_done", "dve_chain", "bank_empty", "pool_done"]]
        con = m["con"]
        ident = con[:, K_ID:K_ID + 128]
        block = ctx.enter_context(nc.Block())

        @block.sync
        def _(sp):
            sp.dma_start(c_sb[:, 0, :], io["L0_c"]).then_inc(s_c, 16)
            sp.dma_start(c_sb[:, 1, :], io["L1_c"]).then_inc(s_c, 16)
            sp.dma_start(con[:], io["constants"]).then_inc(s_small, 16)
            sp.dma_start(wmod[0][:], io["L0_wmod"]).then_inc(s_wm, 16)
            sp.dma_start(m["x"][:], io["L0_attn_x"].rearrange("b (t p) f -> p (b t) f", p=P)).then_inc(loads["x"], 16)
            sp.dma_start(m["wq0"][:], io["L0_attn_wq"]).then_inc(s_w0, 16)
            sp.dma_start(gcol[:, 0:1], io["L0_attn_gate_local_w"].rearrange("h (d a) -> (h d) a", a=1)).then_inc(s_w0, 16)
            sp.dma_start(gcol[:, 1:2], io["L0_attn_gate_remote_w"].rearrange("h (d a) -> (h d) a", a=1)).then_inc(s_w0, 16)
            sp.dma_start(m["wk0"][:], io["L0_attn_wk"]).then_inc(s_w0, 16)
            sp.dma_start(m["wv0"][:], io["L0_attn_wv"]).then_inc(s_w0, 16)
            sp.dma_start(m["wgq"][:], io["L0_attn_wgq"]).then_inc(s_w0, 16)
            sp.dma_start(m["wgk"][:], io["L0_attn_wgk"]).then_inc(s_w0, 16)
            sp.dma_start(m["wgv"][:], io["L0_attn_wgv"]).then_inc(s_w0, 16)
            sp.dma_start(m["rout"][:], io["L0_attn_r_out_w"]).then_inc(s_w0, 16)
            sp.dma_start(m["wo0"][:], io["L0_attn_w_out"]).then_inc(s_w0, 16)
            sp.dma_start(b1row[:], io["L0_ffn_b1"].rearrange("e (c p) -> (e c) p", p=P)).then_inc(s_w0, 16)
            sp.wait_ge(s_w0, 16 * 15)
            sp.wait_ge(loads["x"], 16)

        @block.scalar
        def _(act):
            act.dma_start(wmod[1][:], io["L1_wmod"]).then_inc(s_wm, 16)
            for i, n in enumerate(["Wq", "Wk", "Wv", "Wo"]):
                act.dma_start(wraw[:, i, :], io["L1_attn_" + n]).then_inc(s_w0, 16)
            act.dma_start(m["w1"][:], io["L0_ffn_W1"].rearrange("e f n -> f e n")).then_inc(loads["ffn"], 16)
            act.dma_start(m["w2"][:], io["L0_ffn_W2"].rearrange("e (c p) f -> p (e c) f", p=P)).then_inc(loads["ffn"], 16)
            act.dma_start(m["wg"][:], io["L0_ffn_Wg"]).then_inc(loads["ffn"], 16)
            act.dma_start(m["bg"][:], io["L0_ffn_bg"].rearrange("(a e) -> a e", a=1)).then_inc(loads["ffn"], 16)
            act.dma_start(m["b2"][:], io["L0_ffn_b2"]).then_inc(loads["ffn"], 16)
            for i, n in enumerate(["w_gate", "w_up"]):
                act.dma_start(m["wraw1"][:, i, 0:2, :], io["L1_ffn_" + n][0:256, :].rearrange("(k p) f -> p k f", p=P)).then_inc(loads["q"], 16)
                act.dma_start(m["wraw1"][0:96, i, 2, :], io["L1_ffn_" + n][256:FH, :]).then_inc(loads["q"], 16)
            act.dma_start(m["wraw2"][:], io["L1_ffn_w_down"]).then_inc(loads["q"], 16)
            act.wait_ge(s_c, 32)
            nc.scalar.activation(c_exp[:], c_sb[:], ACT.Exp, scale=-1.0).then_inc(s_exp, 1)
            for b in range(B):
                act.wait_ge(s_pe, 8 + 2 * b)
                nc.scalar.copy(m["gates0"][:, b, :], ps[2 * (b % 2)][:, 0:256]).then_inc(s_act, 1)
                act.wait_ge(s_pe, 9 + 2 * b)
                nc.scalar.copy(m["rows1"][:, b, :], ps[2 * (b % 2) + 1][:, :]).then_inc(s_act, 1)

        @block.gpsimd
        def _(pool):
            link = Chain(pool, s_pool)
            nc.gpsimd.memset(m["hT"][:], 0.0)
            nc.gpsimd.memset(m["mhalf"][:], -0.5)
            for k in range(2):
                nc.gpsimd.memset(m["V"][k][:], 0.0)
                last = nc.gpsimd.memset(m["GV"][k][:], 0.0)
            link(last)
            link(nc.gpsimd.memset(m["ones"][:], 1.0))
            link(nc.gpsimd.memset(m["wraw1"][96:128, :, 2, :], 0.0))
            for r in range(2):
                for k in range(2):
                    nc.gpsimd.memset(m["V0"][k][64 * r:64 * r + 64, :, :, 9 * r + 8:9 * r + 9], 1.0)
                    last = nc.gpsimd.memset(m["GV"][k][64 * r:64 * r + 64, :, 9 * r + 8:9 * r + 9], 1.0)
                link(last)

        @block.vector
        def _(dve):
            link = Chain(dve, s_chain)
            dve.wait_ge(s_exp, 1)
            link(nc.vector.tensor_scalar_add(c_sig[:], c_exp[:], 1.0))
            link(nc.vector.reciprocal(c_exp[:], c_sig[:]))
            nc.vector.tensor_tensor(c_silu[:], c_sb[:], c_exp[:], ALU.mult).then_inc(s_dve, 1)
            dve.wait_ge(s_pe, 1)
            nc.vector.tensor_copy(cT[:], ps[4][:, 0:2 * B].rearrange("p (l b) -> p l b", l=2)).then_inc(s_dve, 1)
            dve.wait_ge(s_pe, 2)
            for i in range(2):
                link(nc.vector.tensor_copy(m["modT"][:, i], ps[5][:, 48 * i:48 * i + 48].rearrange("p (j b) -> p j b", b=B)))
                link(nc.vector.tensor_scalar_add(m["modT"][:, i, 1:5:3, :], m["modT"][:, i, 1:5:3, :], 1.0))
            dve.wait_ge(s_pe, 3)
            for i in range(2):
                for j in range(2):
                    link(nc.vector.tensor_copy(mod8[:, i, 384 * j:384 * j + 384], ps[6 if j == 0 else 7][0:B, :384] if i == 0 else ps[2 * j][0:B, :384]))
            gate = mod8[:].rearrange("p l (a j c) -> p (l a) j c", a=2, j=3)[:, :, 2, :]
            sg, ab = (t[:].rearrange("p l a c -> p (l a) c") for t in (gsgn, gabs))
            link(nc.vector.tensor_scalar(sg, gate, 0.0, 2.0, ALU.is_ge, ALU.mult))
            link(nc.vector.tensor_scalar_add(sg, sg, -1.0))
            link(nc.vector.tensor_tensor(ab, gate, sg, ALU.mult))
            link(nc.vector.scalar_tensor_tensor(gate, ab, 0.25, sg, ALU.max, ALU.mult))
            nc.vector.tensor_scalar_add(mod8[:, 1, 4 * C:5 * C], mod8[:, 1, 4 * C:5 * C], 1.0).then_inc(s_dve, 1)
            dve.wait_ge(s_small, 16)
            nc.vector.tensor_copy(m["identb"][:], ident)
            nc.vector.tensor_copy(m["maskb"][:], con[:, K_LOC0:K_Q0])
            dve.wait_ge(s_w0, 16 * 15)
            dve.wait_ge(s_pe, 4)
            nc.vector.tensor_copy(wqT0[:], ps[4][:, 0:128])
            for i in range(2):
                last = nc.vector.tensor_scalar(G[:, i, :], con[:, K_H:K_H + H], gcol[:, i:i + 1], None, ALU.mult)
            last.then_inc(s_dve, 1)
            for p in range(4):
                for j in range(4):
                    nc.vector.tensor_copy(m["WqD0"][:, p, j, :], m["wq0"][:, 32 * p:32 * p + 32])
            dve.wait_ge(s_pe, 5)
            nc.vector.tensor_copy(m["WG"][:], ps[5][:, 0:32])
            dve.wait_ge(s_pe, 6)
            for j in range(2):
                nc.vector.tensor_copy(m["WqD1"][:, :, j, :], ps[6][:, 0:128].rearrange("p (g f) -> p g f", g=2))
            nc.vector.tensor_copy(m["w1T"][:], ps[6][:, 128:512].rearrange("p (w f) -> p w f", w=3))
            dve.wait_ge(s_pe, 7)
            nc.vector.tensor_copy(m["b1T"][:], ps[7][:, 0:E * HC]).then_inc(s_dve, 1)
            dve.wait_ge(s_dve, 5)

        @block.tensor
        def _(pe):
            pe.wait_ge(s_small, 16)
            pe.wait_ge(s_dve, 1)
            for i in range(2):
                last = nc.tensor.transpose(ps[4][:, B * i:B * i + B], c_silu[:, i, :], con[0:B, 0:B])
            last.then_inc(s_pe, 1)
            pe.wait_ge(s_dve, 2)
            pe.wait_ge(s_wm, 32)
            for i in range(2):
                for j in range(6):
                    last = nc.tensor.matmul(ps[5][:, 48 * i + B * j:48 * i + B * j + B], wmod[i][:, C * j:C * j + C], cT[:, i, :],
                                            start=True, stop=True)
            last.then_inc(s_pe, 1)
            for i in range(2):
                for j in range(2):
                    bank = ps[6 + j] if i == 0 else ps[2 * j]
                    last = nc.tensor.matmul(bank[0:B, 0:384], cT[:, i, :], wmod[i][:, 384 * j:384 * j + 384], start=True, stop=True)
            last.then_inc(s_pe, 1)
            pe.wait_ge(s_w0, 16 * 15)
            nc.tensor.transpose(ps[4][:, 0:128], m["wq0"][:], ident).then_inc(s_pe, 1)
            pe.wait_ge(s_dve, 4)
            nc.tensor.matmul(ps[5][:, 0:32], wqT0[:], G[:].rearrange("p a h -> p (a h)"), start=True, stop=True).then_inc(s_pe, 1)
            for i in range(4):
                last = nc.tensor.transpose(ps[6][:, 128 * i:128 * i + 128], wraw[:, i, :], ident)
            last.then_inc(s_pe, 1)
            nc.tensor.transpose(ps[7][:, 0:E * HC], b1row[:], con[0:E * HC, 0:E * HC]).then_inc(s_pe, 1)
            for b in range(B):
                pick = con[0:B, K_SEL + 128 * b:K_SEL + 128 * b + 128]
                if b >= 2:
                    pe.wait_ge(s_act, 2 * (b - 1))
                for j in range(2):
                    last = nc.tensor.matmul(ps[2 * (b % 2)][:, 128 * j:128 * j + 128], pick, mod8[:, 0, 384 * j + 256:384 * j + 384],
                                            start=True, stop=True)
                last.then_inc(s_pe, 1)
                nc.tensor.matmul(ps[2 * (b % 2) + 1][:, :], pick, mod8[:, 1, 256:768], start=True, stop=True).then_inc(s_pe, 1)
            pe.wait_ge(s_act, 2 * B)


def attention(nc, m, layer):
    L0 = layer == 0
    W = 32 if L0 else 64
    J = P // W
    KW = 2 * W
    FR = P // J
    NP = C // FR
    NU = 6 if L0 else 8
    NT = NU // T
    NF = 8 if L0 else 4
    NTJ = 4 if L0 else 2
    NTE = NTJ - 1
    scale = float(HD) ** -0.5
    with ExitStack() as ctx:
        def sb(name, shape, dt=F32):
            return ctx.enter_context(nc.sbuf_tensor(f"a{layer}_{name}", shape, dt))

        def pb(name):
            return ctx.enter_context(nc.psum_tensor(f"a{layer}_{name}", [P, 512], F32))

        def sem(name):
            return ctx.enter_context(nc.semaphore(f"a{layer}_{name}"))

        stats = sb("stats", [P, T, 6])
        mv = sb("mv", [P, T, 2])
        veps = sb("veps", [P, T])
        rstd = sb("rstd", [P, T])
        xn = sb("xn", [P, T, C])
        Km = [sb(f"Km{k}", [P, NP * T, 4, KW]) for k in range(2)]
        prob = sb("prob", [P, 4, 512])
        nmax = sb("nmax", [P, 2, 8])
        pT = sb("pT", [P, 2, 512])
        Osel = sb("Osel", [P, T, H, 9])
        rec = sb("rec", [P, T, H])
        comb = sb("comb", [P, T, C])
        combT = sb("combT", [P, T, P])
        yg = sb("yg", [P, T, C])
        if L0:
            pool4 = sb("pool4", [P, 2, NLAT])
            hT2 = sb("hT2", [P, 8, 2, KW])
            GQT = [sb(f"GQT{k}", [64, T, P]) for k in range(2)]
            GKm = [sb(f"GKm{k}", [64, LATH, NLAT]) for k in range(2)]
            gz = [sb(f"gz{k}", [P, T, 2, H]) for k in range(2)]
            gsig = sb("gsig", [P, T, 2, H])
            recl = sb("recl", [P, LATH])
            rem = sb("rem", [P, T, 64])
            remT = sb("remT", [64, T, P])
            local = sb("local", [P, T, C])
            remote = sb("remote", [P, T, C])
        hT, Qbd, V, GV, con, identb, modT, x = (m[k] for k in ["hT", "Qbd", "V0" if L0 else "V1", "GV", "con", "identb", "modT", "x"])
        wk, wv = (m["wk0"], m["wv0"]) if L0 else (m["w1T"][:, 0, :], m["w1T"][:, 1, :])
        wo = m["wo0"][:] if L0 else m["w1T"][:, 2, :]
        WqD = m["WqD0" if L0 else "WqD1"]
        gates_b = m["gates0"] if L0 else m["rows1"]
        ident = con[:, K_ID:K_ID + 128]
        bankS = [pb("S0"), pb("S1")]
        bankT = [pb("T0"), pb("T1")]
        bankO = [pb("O0"), pb("O1")]
        bankF, bankY = pb("F"), pb("Y")
        s_scores, s_shift, s_prob, s_tr, s_pT, s_pv, s_oev = [sem(n) for n in [
            "scores_ready", "shifted", "probs_ready", "probs_transposed", "pT_ready", "pv_done", "O_read"]]
        s_ff, s_fe, s_tf, s_te = [sem(n) for n in ["front_filled", "front_read", "tail_filled", "tail_read"]]
        s_mv, s_rstd, s_xn, s_pool4, s_rem, s_comb, s_yg, s_x, s_loc, s_v1, s_h2 = [sem(n) for n in [
            "stats_ready", "rstd_ready", "xn_ready", "pooled_ready", "rem_ready", "comb_ready", "y_ready", "x_updated",
            "local_done", "ones_set", "windows_ready"]]
        s_dch, s_pch, s_ach = sem("dve_chain"), sem("pool_chain"), sem("act_chain")
        block = ctx.enter_context(nc.Block())
        fronts = ([(0, "T"), (1, "K"), (1, "Q0"), (2, "Q1"), (3, "V0"), (3, "V1"), (4, "GB"), (5, "GA")] if L0 else
                  [(0, "T"), (2, "K"), (4, "Q0"), (5, "V0")])
        tails = [(2, "RT"), (3, "R"), (4, "CT"), (5, "Y")] if L0 else [(3, "CT"), (5, "Y")]
        if L0:
            fronts[-1] = (4, "GA")
        job = {name: i for i, (_, name) in enumerate(fronts)}
        tjob = {name: i for i, (_, name) in enumerate(tails)}

        def unit(b, k, lag):
            u = k - lag
            db = 0
            while u < 0:
                u, db = u + NU, db - 1
            while u >= NU:
                u, db = u - NU, db + 1
            return NU * b + (k - lag), b + db, u, db

        @block.gpsimd
        def _(pool):
            link = Chain(pool, s_pch)
            link.per_pair = 2

            def rstd_of(b):
                pool.wait_ge(s_mv, b + 1)
                settle(pool)
                link(nc.gpsimd.tensor_scalar_add(veps[:], mv[:, :, 1], 1e-5))
                nc.gpsimd.tensor_tensor(rstd[:], veps[:], m["mhalf"][:, 0:T], ALU.pow).then_inc(s_rstd, 1)

            def windows_of(b):
                pool.wait_ge(s_fe, NF * b + 1)
                settle(pool)
                for half in range(2):
                    at = PAD - W + W * half
                    last = nc.gpsimd.tensor_copy(hT2[:, :, :, W * half:W * half + W],
                                                 hT[:, at:at + T * P].rearrange("p (w k) -> p w k", k=W).unsqueeze(2)
                                                 .to_broadcast([P, 8, 2, W]))
                last.then_inc(s_h2, 1)

            def slot(b, k, par):
                if k == 0 and has(b, -1, B - 1):
                    rstd_of(b + 1)
                if k == 1 and L0 and has(b, -1, B - 1):
                    windows_of(b + 1)
                if k == NU - 1 and has(b, 1, B + 1):
                    pool.wait_ge(s_yg, b)
                    xt = x[:, bass.ds(T * (b - 1), T), :]
                    nc.gpsimd.tensor_tensor(xt, xt, yg[:], ALU.add).then_inc(s_x, 1)

            def prologue():
                if not L0:
                    for k in range(2):
                        last = nc.gpsimd.memset(m["V"][k][:], 1.0)
                    last.then_inc(s_v1, 1)
                rstd_of(0)
                if L0:
                    windows_of(0)

            run(pool, NU, slot, prologue, [link])

        @block.vector
        def _(dve):
            link = Chain(dve, s_dch)
            link.per_pair = 0

            def stats_of(b):
                wait(dve, s_xn, b)
                for t in range(T):
                    last = nc.vector.bn_stats(stats[:, t, :], x[:, T * b + t, :])
                link(last)
                settle(dve)
                for t in range(T):
                    last = nc.vector.bn_aggr(mv[:, t, :], stats[:, t, :])
                last.then_inc(s_mv, 1)

            def normalise(b):
                dve.wait_ge(s_rstd, b + 1)
                wait(dve, s_ff, NF * (b - 1) + 1)
                for t in range(T):
                    last = nc.vector.tensor_scalar(xn[:, t, :], x[:, T * b + t, :], mv[:, t, 0:1], rstd[:, t:t + 1],
                                                   ALU.subtract, ALU.mult)
                last.then_inc(s_xn, 1)

            def spread_q(b, par, half):
                name = f"Q{half}"
                if not L0:
                    name = "Q0"
                if L0 or half == 0:
                    dve.wait_ge(s_ff, NF * b + job[name] + 1)
                for v in range(2):
                    var = 2 * half + v
                    src = bankF[:, 256 * v:256 * v + 256] if L0 else bankF[:, 256 * half:256 * half + 256]
                    mask = con[:, K_Q0:K_Q0 + 128] if L0 else con[:, K_Q1 + 128 * v:K_Q1 + 128 * v + 128]
                    last = nc.vector.tensor_tensor(Qbd[par][:, var, :, :], src.rearrange("p (t q) -> p t q", t=T),
                                                   mask.unsqueeze(1).to_broadcast([P, T, P]), ALU.mult)
                if L0 or half == 1:
                    last.then_inc(s_fe, 1)

            def move_v(b, par, half):
                dve.wait_ge(s_ff, NF * b + job[f"V{half}"] + 1)
                for r in range(2):
                    last = nc.vector.tensor_copy(
                        V[par][64 * r:64 * r + 64, 4 * half:4 * half + 4, :, 9 * r:9 * r + 8],
                        bankF[64 * r:64 * r + 64, :].rearrange("p (w a r d) -> p w a r d", w=4, r=2, d=HD)[:, :, :, r, :])
                last.then_inc(s_fe, 1)

            def latents(b, par):
                dve.wait_ge(s_ff, NF * b + job["GB"] + 1)
                nc.vector.tensor_tensor(GKm[par][:], bankF[0:64, 0:NLAT].unsqueeze(1).to_broadcast([64, LATH, NLAT]),
                                        con[0:64, K_GK:K_GK + LATH].unsqueeze(2).to_broadcast([64, LATH, NLAT]), ALU.mult)
                for r in range(2):
                    last = nc.vector.tensor_scalar(
                        GV[par][64 * r:64 * r + 64, :, 9 * r:9 * r + 8],
                        bankF[64 * r:64 * r + 64, 64:128].rearrange("p (a r d) -> p a r d", r=2, d=HD)[:, :, r, :],
                        0.25, None, ALU.mult)
                last.then_inc(s_fe, 1)

            def softmax_shift(n, u):
                heads = 8 if L0 else 4
                dve.wait_ge(s_scores, n + 1)
                s3 = bankS[u % 2][:].rearrange("p (h k) -> p h k", h=heads)
                mx = nmax[:, u % 2, 0:heads]
                link(nc.vector.tensor_reduce(mx, s3, AX, ALU.max))
                wait(dve, s_tr, n - 3)
                nc.vector.tensor_tensor(prob[:, u % 4, :].rearrange("p (h k) -> p h k", h=heads), s3,
                                        mx.unsqueeze(2).to_broadcast([P, heads, 512 // heads]), ALU.subtract).then_inc(s_shift, 1)

            def read_o(n, b, u):
                t = u // NT
                if not L0:
                    if u % NT != NT - 1:
                        return
                    dve.wait_ge(s_pv, n + 1)
                    for j in range(J):
                        o = bankO[t][W * j:W * j + W, 0:H * 18].rearrange("p (h j e) -> p h j e", j=J, e=9)[:, :, j, :]
                        last = nc.vector.tensor_copy(Osel[W * j:W * j + W, t, :, :], o)
                    last.then_inc(s_oev, 1)
                    return
                dve.wait_ge(s_pv, n + 1)
                if u % NT == 2:
                    o = bankO[u % 2][:, 0:72].rearrange("p (h e) -> p h e", e=9)
                    link(nc.vector.reciprocal(recl[:], o[:, :, 8]))
                    wait(dve, s_tf, NTJ * (b - 1) + 1)
                    nc.vector.tensor_tensor(rem[:, t, :].rearrange("p (h d) -> p h d", d=HD), o[:, :, 0:8],
                                            recl[:].unsqueeze(2).to_broadcast([P, LATH, HD]), ALU.mult).then_inc(s_oev, 1)
                    return
                for j in range(J):
                    o = bankO[u % 2][W * j:W * j + W, 0:288].rearrange("p (a j e) -> p a j e", j=J, e=18)[:, :, j, :]
                    dst = Osel[W * j:W * j + W, t, 8 * (u % NT):8 * (u % NT) + 8, :].rearrange("p (a r) e -> p a (r e)", r=2)
                    last = nc.vector.tensor_copy(dst, o)
                last.then_inc(s_oev, 1)

            def combine(b, par):
                dve.wait_ge(s_oev, NO_all * (b + 1))
                link(nc.vector.reciprocal(rec[:], Osel[:, :, :, 8]))
                if L0:
                    dve.wait_ge(s_fe, NF * b + job["GA"] + 1)
                    link(nc.vector.tensor_scalar_add(gsig[:], gz[par][:], 1.0))
                    link(nc.vector.reciprocal(gsig[:], gsig[:]))
                    nc_last = nc.vector.tensor_tensor(rec[:], rec[:], gsig[:, :, 0, :], ALU.mult)
                    link(nc_last)
                dst = local if L0 else comb
                ins = nc.vector.tensor_tensor(dst[:].rearrange("p t (h d) -> p (t h) d", d=HD),
                                              Osel[:, :, :, 0:8].rearrange("p t h d -> p (t h) d"),
                                              rec[:].rearrange("p t h -> p (t h)").unsqueeze(2).to_broadcast([P, T * H, HD]), ALU.mult)
                ins.then_inc(s_loc if L0 else s_comb, 1)

            def add_remote(b):
                dve.wait_ge(s_tf, NTJ * b + tjob["R"] + 1)
                nc.vector.tensor_tensor(remote[:].rearrange("p t (h d) -> p t h d", d=HD),
                                        bankY[:, 0:256].rearrange("p (t h d) -> p t h d", t=T, d=HD),
                                        gsig[:, :, 1, :].unsqueeze(3).to_broadcast([P, T, H, HD]), ALU.mult).then_inc(s_te, 1)
                dve.wait_ge(s_te, NTE * b + tjob["R"] + 1)
                dve.wait_ge(s_loc, b + 1)
                nc.vector.tensor_tensor(comb[:], local[:], remote[:], ALU.add).then_inc(s_comb, 1)

            def gate_y(b):
                dve.wait_ge(s_tf, NTJ * b + tjob["Y"] + 1)
                wait(dve, s_x, b)
                nc.vector.tensor_tensor(yg[:], bankY[:, 0:256].rearrange("p (t c) -> p t c", t=T),
                                        gates_b[:, b, 0:C].unsqueeze(1).to_broadcast([P, T, C]), ALU.mult).then_inc(s_yg, 1)

            def slot(b, k, par):
                n, ub, u, _ = unit(b, k, 0)
                if has(b, 0, B):
                    softmax_shift(n, u)
                if k == 0 and has(b, -1, B - 1):
                    normalise(b + 1)
                n2, ub2, u2, db2 = unit(b, k, 2)
                if has(ub2, 0, B):
                    read_o(n2, ub2, u2)
                if k == 1 and has(b, 1, B + 1):
                    combine(b - 1, 1 - par)
                if k == 4 and L0 and has(b, 1, B + 1):
                    add_remote(b - 1)
                if has(b, 0, B - 1):
                    for i, (at, name) in enumerate(fronts):
                        if at != k:
                            continue
                        if name == "Q0":
                            spread_q(b + 1, 1 - par, 0)
                            if not L0:
                                spread_q(b + 1, 1 - par, 1)
                        if name == "Q1":
                            spread_q(b + 1, 1 - par, 1)
                        if name[0] == "V" and L0:
                            move_v(b + 1, 1 - par, int(name[1]))
                        if name == "GB":
                            latents(b + 1, 1 - par)
                    if L0 and k == 1:
                        dve.wait_ge(s_fe, NF * (b + 1) + 1)
                        link(nc.vector.tensor_reduce(pool4[:, 0, :], hT[:, PAD:PAD + T * P].rearrange("p (n c) -> p n c", c=4), AX, ALU.add))
                        nc.vector.tensor_copy(pool4[:, 1, :], pool4[:, 0, :]).then_inc(s_pool4, 1)
                if has(b, 1, B + 1):
                    if k == NU - 1:
                        gate_y(b - 1)
                if k == NU - 1 and has(b, -1, B - 2):
                    stats_of(b + 2)

            NO_all = NU if L0 else T

            def prologue():
                dve.wait_ge(m["ld_x"], 16)
                stats_of(0)
                normalise(0)
                if L0:
                    dve.wait_ge(s_fe, 1)
                    link(nc.vector.tensor_reduce(pool4[:, 0, :], hT[:, PAD:PAD + T * P].rearrange("p (n c) -> p n c", c=4), AX, ALU.add))
                    nc.vector.tensor_copy(pool4[:, 1, :], pool4[:, 0, :]).then_inc(s_pool4, 1)
                spread_q(0, 0, 0)
                spread_q(0, 0, 1)
                if L0:
                    move_v(0, 0, 0)
                    move_v(0, 0, 1)
                    latents(0, 0)
                stats_of(1)

            link.per_pair = 2 * (NU + 1 + (4 + 2 + 1 if L0 else 1))
            run(dve, NU, slot, prologue, [link])

        @block.scalar
        def _(act):
            def feed_h(b):
                act.wait_ge(s_ff, NF * b + 1)
                nc.scalar.activation(hT[:, PAD:PAD + T * P], bankF[:, 0:T * P], ACT.Identity,
                                     bias=modT[:, layer, 0, bass.ds(b, 1)], scale=modT[:, layer, 1, bass.ds(b, 1)]).then_inc(s_fe, 1)

            def spread_k(b, par):
                act.wait_ge(s_ff, NF * b + job["K"] + 1)
                for s in range(4):
                    last = nc.scalar.activation(Km[par][:, :, s, :], bankF[:].rearrange("p (g k) -> p g k", k=KW), ACT.Copy,
                                                scale=con[:, K_S + s:K_S + s + 1])
                last.then_inc(s_fe, 1)

            def move_v(b, par):
                act.wait_ge(s_ff, NF * b + job["V0"] + 1)
                nc.scalar.copy(V[par][:].rearrange("p w h e -> p (w h) e")[:, :, 0:8],
                               bankF[:].rearrange("p (g d) -> p g d", d=HD)).then_inc(s_fe, 1)

            def latent_q(b, par):
                act.wait_ge(s_ff, NF * b + job["GA"] + 1)
                nc.scalar.activation(GQT[par][:], bankF[0:64, 0:256].rearrange("p (t q) -> p t q", t=T), ACT.Copy, scale=scale)
                wait(act, s_loc, b - 1)
                nc.scalar.activation(gz[par][:], bankF[:, 256:320].rearrange("p (t a h) -> p t a h", t=T, a=2), ACT.Exp,
                                     scale=-1.0).then_inc(s_fe, 1)

            def slot(b, k, par):
                n1, ub1, u1, _ = unit(b, k, 1)
                if has(ub1, 0, B):
                    act.wait_ge(s_tr, n1 + 1)
                    wait(act, s_pv, n1 - 1)
                    nc.scalar.copy(pT[:, u1 % 2, :], bankT[u1 % 2][:]).then_inc(s_pT, 1)
                if has(b, 0, B):
                    n, _, u, _ = unit(b, k, 0)
                    act.wait_ge(s_shift, n + 1)
                    nc.scalar.activation(prob[:, u % 4, :], prob[:, u % 4, :], ACT.Exp).then_inc(s_prob, 1)
                if has(b, 1, B + 1):
                    for at, name in tails:
                        if at != k or name in ("R", "Y"):
                            continue
                        act.wait_ge(s_tf, NTJ * (b - 1) + tjob[name] + 1)
                        dst, rows = (remT, 64) if name == "RT" else (combT, P)
                        nc.scalar.copy(dst[:], bankY[0:rows, 0:256].rearrange("p (t q) -> p t q", t=T)).then_inc(s_te, 1)
                if has(b, 0, B - 1):
                    for at, name in fronts:
                        if at == k:
                            if name == "T":
                                feed_h(b + 1)
                            if name == "K":
                                spread_k(b + 1, 1 - par)
                            if name == "V0" and not L0:
                                move_v(b + 1, 1 - par)
                            if name == "GA":
                                latent_q(b + 1, 1 - par)

            def prologue():
                feed_h(0)
                spread_k(0, 0)
                if L0:
                    latent_q(0, 0)
                else:
                    act.wait_ge(s_v1, 1)
                    move_v(0, 0)

            run(act, NU, slot, prologue)

        @block.tensor
        def _(pe):
            def front(b, par, name):
                i = job[name]
                wait(pe, s_fe, NF * b + i)
                if name == "T":
                    pe.wait_ge(s_xn, b + 1)
                    for t in range(T):
                        last = nc.tensor.transpose(bankF[:, P * t:P * t + P], xn[:, t, :], ident)
                elif name == "K":
                    for p in range(NP):
                        for j in range(J):
                            at = PAD + W * (j - 1)
                            rhs = hT[:, at:at + T * P].rearrange("p (t q) -> p t q", t=T)[:, :, 0:KW]
                            last = nc.tensor.matmul(bankF[FR * j:FR * j + FR, T * KW * p:T * KW * (p + 1)],
                                                    wk[:, FR * p:FR * p + FR], rhs, start=True, stop=True)
                elif name[0] == "Q":
                    half = int(name[1])
                    for v in range(2):
                        p = 2 * half + v
                        last = nc.tensor.matmul(bankF[:, 256 * v:256 * v + 256], WqD[:, p, :, :].rearrange("p j f -> p (j f)"),
                                                hT[:, PAD:PAD + T * P], start=True, stop=True)
                elif name[0] == "V":
                    for w in range(4):
                        win = 4 * int(name[1]) + w
                        at = PAD + W * (win - 1)
                        if L0:
                            pe.wait_ge(s_h2, b + 1)
                            lhsT = hT2[:, win].rearrange("p r k -> p (r k)")
                        else:
                            lhsT = hT[:, at:at + KW]
                        last = nc.tensor.matmul(bankF[:, C * w:C * w + C], lhsT, wv[:] if L0 else wv, start=True, stop=True)
                elif name == "GB":
                    pe.wait_ge(s_pool4, b + 1)
                    nc.tensor.matmul(bankF[0:64, 0:NLAT], m["wgk"][:], pool4[:, 0, :], start=True, stop=True)
                    last = nc.tensor.matmul(bankF[:, 64:128], pool4[:].rearrange("p a n -> p (a n)"), m["wgv"][:],
                                            start=True, stop=True)
                elif name == "GA":
                    nc.tensor.matmul(bankF[0:64, 0:256], m["wgq"][:], hT[:, PAD:PAD + T * P], start=True, stop=True)
                    for t in range(T):
                        last = nc.tensor.matmul(bankF[:, 256 + 32 * t:288 + 32 * t], hT[:, PAD + P * t:PAD + P * t + P], m["WG"][:],
                                                start=True, stop=True)
                last.then_inc(s_ff, 1)

            def tail(b, name):
                i = tjob[name]
                if i == 0:
                    wait(pe, s_yg, b)
                else:
                    pe.wait_ge(s_te, NTE * b + i)
                if name == "RT":
                    pe.wait_ge(s_oev, NU * (b + 1))
                    settle(pe)
                    for t in range(T):
                        last = nc.tensor.transpose(bankY[0:64, P * t:P * t + P], rem[:, t, :], ident)
                elif name == "R":
                    for t in range(T):
                        last = nc.tensor.matmul(bankY[:, C * t:C * t + C], remT[:, t, :], m["rout"][:], start=True, stop=True)
                elif name == "CT":
                    pe.wait_ge(s_comb, b + 1)
                    for t in range(T):
                        last = nc.tensor.transpose(bankY[:, P * t:P * t + P], comb[:, t, :], ident)
                else:
                    for t in range(T):
                        last = nc.tensor.matmul(bankY[:, C * t:C * t + C], combT[:, t, :], wo, start=True, stop=True)
                last.then_inc(s_tf, 1)

            def scores(n, b, u, par):
                t, g = u // NT, u % NT
                if u == 0:
                    pe.wait_ge(s_fe, NF * (b + 1))
                wait(pe, s_shift, n - 1)
                bank = bankS[u % 2]
                if L0 and g == 2:
                    mask = m["maskb"][:, 128 + 64 * t:192 + 64 * t].unsqueeze(1).to_broadcast([P, LATH, NLAT])
                elif L0:
                    mask = m["maskb"][:, 64 * t:64 * t + 64].unsqueeze(1).to_broadcast([P, 4, KW])
                else:
                    mask = m["maskb"][:, 256 + 128 * t:384 + 128 * t].unsqueeze(1).to_broadcast([P, 4, KW])
                if not L0 or g == 2:
                    nc.tensor.matmul(bank[:], identb[:], mask, start=True, stop=False)
                if L0 and g == 2:
                    last = nc.tensor.matmul(bank[:], GQT[par][:, t, :], GKm[par][:].rearrange("p h n -> p (h n)"), start=False, stop=True)
                elif L0:
                    for i in range(2):
                        p = 2 * g + i
                        nc.tensor.matmul(bank[:, 256 * i:256 * i + 256], identb[:], mask, start=True, stop=False)
                        last = nc.tensor.matmul(bank[:, 256 * i:256 * i + 256], Qbd[par][:, p, t, :],
                                                Km[par][:, T * p + t, :, :].rearrange("p s k -> p (s k)"), start=False, stop=True)
                else:
                    last = nc.tensor.matmul(bank[:], Qbd[par][:, g, t, :],
                                            Km[par][:, T * (g // 2) + t, :, :].rearrange("p s k -> p (s k)"), start=False, stop=True)
                last.then_inc(s_scores, 1)

            def turn(n, u):
                pe.wait_ge(s_prob, n + 1)
                wait(pe, s_pT, n - 1)
                for i in range(4):
                    last = nc.tensor.transpose(bankT[u % 2][:, P * i:P * i + P], prob[:, u % 4, P * i:P * i + P], ident)
                last.then_inc(s_tr, 1)

            def values(n, b, u, par):
                t, g = u // NT, u % NT
                pe.wait_ge(s_pT, n + 1)
                if L0:
                    wait(pe, s_oev, n - 1)
                elif g == 0:
                    wait(pe, s_oev, T * b + t - 1)
                for i in range(4):
                    lhsT = pT[:, u % 2, P * i:P * i + P]
                    if L0 and g == 2:
                        out, rhs = bankO[u % 2][:, 18 * i:18 * i + 18], GV[par][:, i, :]
                    elif L0:
                        out, rhs = bankO[u % 2][:, 72 * i:72 * i + 72], V[par][:, 4 * t:4 * t + 4, 4 * g + i, :]
                    else:
                        h = 4 * g + i
                        out, rhs = bankO[t][:, 18 * h:18 * h + 18], V[par][:, 2 * t:2 * t + 2, h, :]
                    last = nc.tensor.matmul(out, lhsT, rhs, start=True, stop=True)
                last.then_inc(s_pv, 1)

            def slot(b, k, par):
                n1, ub1, u1, _ = unit(b, k, 1)
                if has(ub1, 0, B):
                    turn(n1, u1)
                nn, ubn, un, dbn = unit(b, k, -1)
                if has(ubn, 0, B):
                    scores(nn, ubn, un, (par + dbn) % 2)
                n2, ub2, u2, db2 = unit(b, k, 2)
                if has(ub2, 0, B):
                    values(n2, ub2, u2, (par + db2) % 2)
                if has(b, 1, B + 1):
                    for at, name in tails:
                        if at == k:
                            tail(b - 1, name)
                if has(b, 0, B - 1):
                    for at, name in fronts:
                        if at == k:
                            front(b + 1, 1 - par, name)

            def prologue():
                for _, name in fronts:
                    front(0, 0, name)
                scores(0, 0, 0, 0)

            run(pe, NU, slot, prologue)


def build(nc, io, out):
    with ExitStack() as ctx:
        def sb(name, shape, dt=F32):
            return ctx.enter_context(nc.sbuf_tensor(name, shape, dt))

        m = {
            "con": sb("con", [P, K_END]), "identb": sb("identb", [P, P], BF16), "maskb": sb("maskb", [P, K_Q0 - K_LOC0], BF16),
            "x": sb("x", [P, B * T, C]), "modT": sb("modT", [P, 2, 6, B]),
            "gates0": sb("gates0", [P, B, 2 * C]), "rows1": sb("rows1", [P, B, 4 * C]),
            "wq0": sb("wq0", [P, C]), "wk0": sb("wk0", [P, C]), "wv0": sb("wv0", [P, C]), "wo0": sb("wo0", [P, C]),
            "wgq": sb("wgq", [P, 64]), "wgk": sb("wgk", [P, 64]), "wgv": sb("wgv", [P, 64]), "rout": sb("rout", [64, C]),
            "WG": sb("WG", [P, 32]), "WqD0": sb("WqD0", [P, 4, 4, 32]), "WqD1": sb("WqD1", [P, 2, 2, 64]),
            "w1T": sb("w1T", [P, 3, C]), "b1T": sb("b1T", [P, E * HC]),
            "w1": sb("w1", [P, E, HC * P]), "w2": sb("w2", [P, E * HC, C]), "wg": sb("wg", [P, E]), "bg": sb("bg", [1, E]),
            "b2": sb("b2", [E, C]), "wraw1": sb("wraw1", [P, 2, 3, C]), "wraw2": sb("wraw2", [P, FH]),
            "hT": sb("hT", [P, PAD + T * P + PAD]), "ones": sb("ones", [1, P]), "mhalf": sb("mhalf", [P, 2]),
            "Qbd": [sb(f"Qbd{k}", [P, 4, T, P]) for k in range(2)],
            "V": [sb(f"V{k}", [P, 8 * 8 * 18]) for k in range(2)],
            "GV": [sb(f"GV{k}", [P, 4, 18]) for k in range(2)],
        }
        m["V0"] = [v[:].rearrange("p (w a e) -> p w a e", w=8, e=18) for v in m["V"]]
        m["V1"] = [v[:, 0:4 * H * 9].rearrange("p (w h e) -> p w h e", w=4, e=9) for v in m["V"]]
        loads = {k: ctx.enter_context(nc.semaphore(f"ld_{k}")) for k in ["x", "ffn", "q"]}
        m["ld_x"] = loads["x"]
        setup(nc, io, m, loads)
        attention(nc, m, 0)
        experts(nc, m, loads)
        attention(nc, m, 1)
        quant_ffn(nc, m, loads, out)


def experts(nc, m, loads):
    with ExitStack() as ctx:
        def sb(name, shape, dt=F32):
            return ctx.enter_context(nc.sbuf_tensor(f"e_{name}", shape, dt))

        def pb(name):
            return ctx.enter_context(nc.psum_tensor(f"e_{name}", [P, 512], F32))

        def sem(name):
            return ctx.enter_context(nc.semaphore(f"e_{name}"))

        stats, mv, veps, rstd = sb("stats", [P, T, 6]), sb("mv", [P, T, 2]), sb("veps", [P, T]), sb("rstd", [P, T])
        xn = sb("xn", [P, T, C])
        hTe = [sb(f"hT{k}", [P, T * P]) for k in range(2)]
        hid = [sb(f"hid{k}", [P, HC, T * P]) for k in range(2)]
        acc = [sb(f"acc{k}", [P, T, C]) for k in range(2)]
        sel = [sb(f"sel{k}", [P, T, E]) for k in range(2)]
        b2s = sb("b2s", [P, T, C])
        selT = sb("selT", [E, T * P])
        yg = sb("yg", [P, T, C])
        top, lg, ex, tot = sb("top", [P, T]), sb("lg", [P, T, E]), sb("ex", [P, T, E]), sb("tot", [P, T])
        prb, gt, eq, rank = sb("prb", [P, T, E]), sb("gt", [P, T, E, E]), sb("eq", [P, T, E, E]), sb("rank", [P, T, E])
        bankH = [pb(f"H{c}") for c in range(HC)]
        bankY = [pb("Y0"), pb("Y1")]
        bankF = pb("F")
        x, con, modT = m["x"], m["con"], m["modT"]
        ident = con[:, K_ID:K_ID + 128]
        s_hid, s_gelu, s_y, s_acc, s_ff, s_fe, s_mv, s_rstd, s_xn, s_lg, s_ex, s_sel, s_x, s_dch, s_pch = [sem(n) for n in [
            "hidden_ready", "gelu_done", "y_ready", "accumulated", "front_filled", "front_read", "stats_ready", "rstd_ready",
            "xn_ready", "logits_ready", "exp_ready", "weights_ready", "x_updated", "dve_chain", "pool_chain"]]
        NF = 4
        fronts = [(1, "T"), (2, "G"), (5, "ST"), (6, "B2")]
        job = {name: i for i, (_, name) in enumerate(fronts)}
        block = ctx.enter_context(nc.Block())

        @block.gpsimd
        def _(pool):
            link = Chain(pool, s_pch)
            link.per_pair = 4

            def rstd_of(b):
                pool.wait_ge(s_mv, b + 1)
                settle(pool)
                link(nc.gpsimd.tensor_scalar_add(veps[:], mv[:, :, 1], 1e-5))
                nc.gpsimd.tensor_tensor(rstd[:], veps[:], m["mhalf"][:, 0:T], ALU.pow).then_inc(s_rstd, 1)

            def update(b, par):
                pool.wait_ge(s_acc, E * (b + 1))
                wait(pool, s_x, b)
                link(nc.gpsimd.tensor_tensor(yg[:], acc[par][:], m["gates0"][:, b, C:2 * C].unsqueeze(1).to_broadcast([P, T, C]),
                                             ALU.mult))
                xt = x[:, bass.ds(T * b, T), :]
                nc.gpsimd.tensor_tensor(xt, xt, yg[:], ALU.add).then_inc(s_x, 1)

            def slot(b, k, par):
                if k == 0 and has(b, 1, B + 1):
                    update(b - 1, 1 - par)
                if k == 7 and has(b, -1, B - 2):
                    rstd_of(b + 2)

            def prologue():
                rstd_of(0)
                rstd_of(1)

            run(pool, E, slot, prologue, [link])

        @block.vector
        def _(dve):
            link = Chain(dve, s_dch)
            link.per_pair = 2 * 13

            def stats_of(b):
                wait(dve, s_xn, b)
                for t in range(T):
                    last = nc.vector.bn_stats(stats[:, t, :], x[:, T * b + t, :])
                link(last)
                settle(dve)
                for t in range(T):
                    last = nc.vector.bn_aggr(mv[:, t, :], stats[:, t, :])
                last.then_inc(s_mv, 1)

            def normalise(b):
                dve.wait_ge(s_rstd, b + 1)
                wait(dve, s_ff, NF * (b - 1) + 1)
                for t in range(T):
                    last = nc.vector.tensor_scalar(xn[:, t, :], x[:, T * b + t, :], mv[:, t, 0:1], rstd[:, t:t + 1],
                                                   ALU.subtract, ALU.mult)
                last.then_inc(s_xn, 1)

            def logits(b):
                dve.wait_ge(s_ff, NF * b + job["G"] + 1)
                l3 = bankF[:, 0:T * E].rearrange("p (t e) -> p t e", t=T)
                link(nc.vector.tensor_reduce(top[:], l3, AX, ALU.max))
                nc.vector.tensor_tensor(lg[:], l3, top[:].unsqueeze(2).to_broadcast([P, T, E]), ALU.subtract).then_inc(s_fe, 1)

            def select(b, par):
                dve.wait_ge(s_ex, b + 1)
                link(nc.vector.tensor_reduce(tot[:], ex[:], AX, ALU.add))
                link(nc.vector.reciprocal(tot[:], tot[:]))
                link(nc.vector.tensor_tensor(prb[:], ex[:], tot[:].unsqueeze(2).to_broadcast([P, T, E]), ALU.mult))
                other = prb[:].unsqueeze(2).to_broadcast([P, T, E, E])
                own = prb[:].unsqueeze(3).to_broadcast([P, T, E, E])
                nc.vector.tensor_tensor(gt[:], other, own, ALU.is_gt)
                link(nc.vector.tensor_tensor(eq[:], other, own, ALU.is_equal))
                flat = [P, T, E * E]
                gt2, eq2 = (a[:].rearrange("p t e f -> p t (e f)") for a in (gt, eq))
                link(nc.vector.tensor_tensor(eq2, eq2, con[:, K_TRI:K_TRI + E * E].unsqueeze(1).to_broadcast(flat), ALU.mult))
                link(nc.vector.tensor_tensor(gt2, gt2, eq2, ALU.add))
                link(nc.vector.tensor_reduce(rank[:], gt[:], AX, ALU.add))
                link(nc.vector.scalar_tensor_tensor(prb[:], rank[:], 1.5, prb[:], ALU.is_lt, ALU.mult))
                link(nc.vector.tensor_reduce(tot[:], prb[:], AX, ALU.add))
                link(nc.vector.tensor_scalar_add(tot[:], tot[:], 1e-8))
                link(nc.vector.reciprocal(tot[:], tot[:]))
                nc.vector.tensor_tensor(sel[par][:], prb[:], tot[:].unsqueeze(2).to_broadcast([P, T, E]), ALU.mult).then_inc(s_sel, 1)

            def accumulate(n, b, e, par):
                dve.wait_ge(s_y, n + 1)
                if e == 0:
                    dve.wait_ge(s_fe, NF * (b + 1))
                    wait(dve, s_x, b - 1)
                else:
                    wait(dve, s_acc, n)
                for t in range(T):
                    last = nc.vector.scalar_tensor_tensor(acc[par][:, t, :], bankY[e % 2][:, C * t:C * t + C], sel[par][:, t, e:e + 1],
                                                          b2s[:, t, :] if e == 0 else acc[par][:, t, :], ALU.mult, ALU.add)
                last.then_inc(s_acc, 1)

            def slot(b, k, par):
                if has(b, 0, B - 1):
                    if k == 3:
                        logits(b + 1)
                    if k == 4:
                        select(b + 1, 1 - par)
                if has(b, 0, B):
                    accumulate(E * b + k, b, k, par)
                if k == 0 and has(b, 0, B - 1):
                    normalise(b + 1)
                if k == 6 and has(b, -1, B - 2):
                    stats_of(b + 2)

            def prologue():
                stats_of(0)
                normalise(0)
                logits(0)
                select(0, 0)
                stats_of(1)

            run(dve, E, slot, prologue, [link])

        @block.scalar
        def _(act):
            def feed_h(b, par):
                act.wait_ge(s_ff, NF * b + 1)
                nc.scalar.activation(hTe[par][:], bankF[:, 0:T * P], ACT.Identity,
                                     bias=modT[:, 0, 3, bass.ds(b, 1)], scale=modT[:, 0, 4, bass.ds(b, 1)]).then_inc(s_fe, 1)

            def gelu(n, e, par):
                wait(act, s_y, n - 1)
                for c in range(HC):
                    act.wait_ge(s_hid, HC * n + c + 1)
                    nc.scalar.activation(hid[e % 2][:, c, :], bankH[c][:, 0:T * P], ACT.Gelu_apprx_tanh,
                                         bias=m["b1T"][:, HC * e + c:HC * e + c + 1]).then_inc(s_gelu, 1)

            def fronts_of(b, k, par):
                if k == 1:
                    feed_h(b, par)
                if k == 3:
                    act.wait_ge(s_fe, NF * b + job["G"] + 1)
                    wait(act, s_sel, b)
                    nc.scalar.activation(ex[:], lg[:], ACT.Exp).then_inc(s_ex, 1)
                if k == 5:
                    act.wait_ge(s_ff, NF * b + job["ST"] + 1)
                    nc.scalar.copy(selT[:], bankF[0:E, 0:T * P]).then_inc(s_fe, 1)
                if k == 6:
                    act.wait_ge(s_ff, NF * b + job["B2"] + 1)
                    wait(act, s_acc, E * (b - 1) + 1)
                    nc.scalar.copy(b2s[:], bankF[:, 0:T * C].rearrange("p (t c) -> p t c", t=T)).then_inc(s_fe, 1)

            def slot(b, k, par):
                e, nb = (k + 1) % E, b + (k + 1) // E
                if has(nb, 0, B):
                    gelu(E * b + k + 1, e, par)
                if has(b, 0, B - 1):
                    fronts_of(b + 1, k, 1 - par)

            def prologue():
                for k in (1, 3, 5, 6):
                    fronts_of(0, k, 0)
                gelu(0, 0, 0)

            run(act, E, slot, prologue)

        @block.tensor
        def _(pe):
            def front(b, par, name):
                i = job[name]
                wait(pe, s_fe, NF * b + i)
                if name == "T":
                    pe.wait_ge(s_xn, b + 1)
                    for t in range(T):
                        last = nc.tensor.transpose(bankF[:, P * t:P * t + P], xn[:, t, :], ident)
                elif name == "G":
                    for t in range(T):
                        out = bankF[:, E * t:E * t + E]
                        nc.tensor.matmul(out, hTe[par][:, P * t:P * t + P], m["wg"][:], start=True, stop=False)
                        last = nc.tensor.matmul(out, m["ones"][:], m["bg"][:], start=False, stop=True)
                elif name == "ST":
                    pe.wait_ge(s_sel, b + 1)
                    settle(pe)
                    for t in range(T):
                        last = nc.tensor.transpose(bankF[0:E, P * t:P * t + P], sel[par][:, t, :], ident)
                else:
                    for t in range(T):
                        last = nc.tensor.matmul(bankF[:, C * t:C * t + C], selT[:, P * t:P * t + P], m["b2"][:], start=True, stop=True)
                last.then_inc(s_ff, 1)

            def hidden(n, e, par):
                for c in range(HC):
                    wait(pe, s_gelu, HC * (n - 1) + c + 1)
                    nc.tensor.matmul(bankH[c][:, 0:T * P], m["w1"][:, e, P * c:P * c + P], hTe[par][:], start=True, stop=True)\
                        .then_inc(s_hid, 1)

            def output(n, e):
                pe.wait_ge(s_gelu, HC * (n + 1))
                wait(pe, s_acc, n - 1)
                for t in range(T):
                    for c in range(HC):
                        last = nc.tensor.matmul(bankY[e % 2][:, C * t:C * t + C], hid[e % 2][:, c, P * t:P * t + P],
                                                m["w2"][:, HC * e + c, :], start=c == 0, stop=c == HC - 1)
                last.then_inc(s_y, 1)

            def slot(b, k, par):
                e, db = (k + 1) % E, (k + 1) // E
                if has(b + db, 0, B):
                    if db:
                        pe.wait_ge(s_fe, NF * (b + 1) + 1)
                    hidden(E * b + k + 1, e, (par + db) % 2)
                if has(b, 0, B):
                    output(E * b + k, k)
                if has(b, 0, B - 1):
                    for at, name in fronts:
                        if at == k:
                            front(b + 1, 1 - par, name)

            def prologue():
                pe.wait_ge(loads["ffn"], 16 * 5)
                for _, name in fronts:
                    front(0, 0, name)
                hidden(0, 0, 0)

            run(pe, E, slot, prologue)


RND = [1.5 * 2.0 ** 22, 1.5 * 2.0 ** 23, 1.5 * 2.0 ** 24]
TIE = 1.0 - 2.0 ** -24


class Quantiser:

    def __init__(self, nc, ctx, name, n):
        def sb(s, shape):
            return ctx.enter_context(nc.sbuf_tensor(f"{name}_{s}", shape, F32))
        self.nc, self.n = nc, n
        self.sc, self.rs = sb("sc", [P, n // 16]), sb("rs", [P, n // 16])
        self.v, self.a, self.z1, self.z2, self.z3 = (sb(s, [P, n]) for s in ("v", "a", "z1", "z2", "z3"))
        self.scaled, self.mag, self.parted, self.done = (ctx.enter_context(nc.semaphore(f"{name}_{s}"))
                                                         for s in ("scaled", "magnitudes", "parts", "quantised"))

    def scales(self, link, src, src3):
        v = self.nc.vector
        link(v.tensor_reduce(self.sc[:], src3, AX, ALU.max, apply_absolute_value=True))
        link(v.tensor_scalar(self.sc[:], self.sc[:], 1.0 / 6.0, 1e-12, ALU.mult, ALU.max))
        link(v.reciprocal(self.rs[:], self.sc[:]))
        v.tensor_tensor(self.v[:].rearrange("p (g k) -> p g k", k=16), src3,
                        self.rs[:].unsqueeze(2).to_broadcast([P, self.n // 16, 16]), ALU.mult).then_inc(self.scaled, 1)

    def magnitude(self, act, i):
        act.wait_ge(self.scaled, i + 1)
        wait(act, self.done, i)
        self.nc.scalar.activation(self.a[:], self.v[:], ACT.Abs, scale=TIE).then_inc(self.mag, 1)

    def parts(self, pool, i):
        pool.wait_ge(self.mag, i + 1)
        settle(pool)
        self.nc.gpsimd.tensor_scalar(self.z1[:], self.a[:], RND[0], RND[0] + 2.0, ALU.add, ALU.min)
        self.nc.gpsimd.tensor_scalar(self.z3[:], self.a[:], 4.0, RND[2], ALU.max, ALU.add).then_inc(self.parted, 1)

    def rebuild(self, dve, link, i, out):
        v = self.nc.vector
        dve.wait_ge(self.mag, i + 1)
        link(v.tensor_scalar(self.z2[:], self.a[:], 2.0, RND[1], ALU.max, ALU.add))
        link(v.tensor_scalar(self.z2[:], self.z2[:], RND[1] + 4.0, RND[1] + 2.0, ALU.min, ALU.subtract))
        dve.wait_ge(self.parted, i + 1)
        link(v.scalar_tensor_tensor(self.z2[:], self.z1[:], RND[0], self.z2[:], ALU.subtract, ALU.add))
        link(v.scalar_tensor_tensor(self.z2[:], self.z3[:], RND[2] + 4.0, self.z2[:], ALU.subtract, ALU.add))
        link(v.tensor_tensor(self.z2[:].rearrange("p (g k) -> p g k", k=16), self.z2[:].rearrange("p (g k) -> p g k", k=16),
                             self.sc[:].unsqueeze(2).to_broadcast([P, self.n // 16, 16]), ALU.mult))
        v.scalar_tensor_tensor(out.bitcast(I32), self.v[:].bitcast(I32), -2 ** 31, self.z2[:].bitcast(I32),
                               ALU.bitwise_and, ALU.bitwise_or).then_inc(self.done, 1)


def quant_ffn(nc, m, loads, out):
    with ExitStack() as ctx:
        def sb(name, shape, dt=F32):
            return ctx.enter_context(nc.sbuf_tensor(f"q_{name}", shape, dt))

        def sem(name):
            return ctx.enter_context(nc.semaphore(f"q_{name}"))

        stats, mv, veps, rstd = sb("stats", [P, T, 6]), sb("mv", [P, T, 2]), sb("veps", [P, T]), sb("rstd", [P, T])
        xn, xm, h = sb("xn", [P, T, C]), sb("xm", [P, T, C]), sb("h", [P, T, C])
        hq, hqT = sb("hq", [P, T * C]), sb("hqT", [P, T, P])
        sg, u = sb("sg", [P, T, FH]), sb("u", [P, T * FH])
        uq, uT = sb("uq", [P, T * FH]), sb("uT", [P, T, 3, P])
        yg = sb("yg", [P, T, C])
        wq, wdq = sb("wq", [P, 2 * 3 * C]), sb("wdq", [P, FH])
        wguT, wdT = sb("wguT", [P, 2, 3 * P]), sb("wdT", [P, 3, C])
        gu = ctx.enter_context(nc.psum_tensor("q_gu", [P, 4, 512], F32))
        bankX = ctx.enter_context(nc.psum_tensor("q_X", [P, 512], F32))
        bankU = [ctx.enter_context(nc.psum_tensor(f"q_U{t}", [P, 512], F32)) for t in range(T)]
        bankY = ctx.enter_context(nc.psum_tensor("q_Y", [P, 512], F32))
        guv = gu[:].rearrange("p (t a) k -> p t a k", a=2)
        qw1 = Quantiser(nc, ctx, "qw1", 2 * 3 * C)
        qw2 = Quantiser(nc, ctx, "qw2", FH)
        qx = Quantiser(nc, ctx, "qx", T * C)
        qu = Quantiser(nc, ctx, "qu", T * FH)
        x, con, rows = m["x"], m["con"], m["rows1"]
        ident = con[:, K_ID:K_ID + 128]
        (s_wT, s_wTe, s_xT, s_xTe, s_gu, s_sg, s_u, s_uT, s_uTe, s_y, s_yg, s_x, s_mv, s_rstd, s_xn, s_h, s_out, s_dch,
         s_pch) = [sem(n) for n in ["w_transposed", "w_ready", "x_transposed", "xT_ready", "gate_up_ready", "silu_ready", "u_ready",
                                    "u_transposed", "uT_ready", "y_ready", "yg_ready", "x_updated", "stats_ready", "rstd_ready",
                                    "xn_ready", "h_ready", "stored", "dve_chain", "pool_chain"]]
        block = ctx.enter_context(nc.Block())

        @block.sync
        def _(sp):
            for b in range(B):
                sp.wait_ge(s_x, b + 1)
                sp.dma_start(out[b].rearrange("(t p) f -> p t f", p=P), x[:, T * b:T * b + T, :]).then_inc(s_out, 16)
            sp.wait_ge(s_out, 16 * B)

        @block.gpsimd
        def _(pool):
            link = Chain(pool, s_pch)
            link.per_pair = 4

            def rstd_of(b):
                pool.wait_ge(s_mv, b + 1)
                settle(pool)
                link(nc.gpsimd.tensor_scalar_add(veps[:], mv[:, :, 1], 1e-5))
                nc.gpsimd.tensor_tensor(rstd[:], veps[:], m["mhalf"][:, 0:T], ALU.pow).then_inc(s_rstd, 1)

            def modulate(b):
                pool.wait_ge(s_xn, b + 1)
                wait(pool, s_h, b)
                link(nc.gpsimd.tensor_tensor(xm[:], xn[:], rows[:, b, 2 * C:3 * C].unsqueeze(1).to_broadcast([P, T, C]), ALU.mult))
                wait(pool, qx.scaled, b)
                nc.gpsimd.tensor_tensor(h[:], xm[:], rows[:, b, C:2 * C].unsqueeze(1).to_broadcast([P, T, C]), ALU.add)\
                    .then_inc(s_h, 1)

            def slot(b, k, par):
                if has(b, 0, B - 1):
                    modulate(b + 1)
                    qx.parts(pool, b + 1)
                if has(b, 0, B):
                    qu.parts(pool, b)
                if has(b, -1, B - 2):
                    rstd_of(b + 2)
                if has(b, 0, B):
                    pool.wait_ge(s_yg, b + 1)
                    xt = x[:, bass.ds(T * b, T), :]
                    nc.gpsimd.tensor_tensor(xt, xt, yg[:], ALU.add).then_inc(s_x, 1)

            def prologue():
                rstd_of(0)
                qw1.parts(pool, 0)
                qw2.parts(pool, 0)
                modulate(0)
                rstd_of(1)
                qx.parts(pool, 0)

            run(pool, 1, slot, prologue, [link])

        @block.vector
        def _(dve):
            link = Chain(dve, s_dch)
            link.per_pair = 2 * 17

            def stats_of(b):
                wait(dve, s_xn, b)
                for t in range(T):
                    last = nc.vector.bn_stats(stats[:, t, :], x[:, T * b + t, :])
                link(last)
                settle(dve)
                for t in range(T):
                    last = nc.vector.bn_aggr(mv[:, t, :], stats[:, t, :])
                last.then_inc(s_mv, 1)

            def normalise(b):
                dve.wait_ge(s_rstd, b + 1)
                wait(dve, s_h, b)
                for t in range(T):
                    last = nc.vector.tensor_scalar(xn[:, t, :], x[:, T * b + t, :], mv[:, t, 0:1], rstd[:, t:t + 1],
                                                   ALU.subtract, ALU.mult)
                last.then_inc(s_xn, 1)

            def scale_x(b):
                dve.wait_ge(s_h, b + 1)
                qx.scales(link, h, h[:].rearrange("p t (g k) -> p (t g) k", k=16))

            def rebuild_x(b):
                wait(dve, s_xT, b)
                qx.rebuild(dve, link, b, hq[:])

            def slot(b, k, par):
                if has(b, 0, B - 1):
                    normalise(b + 1)
                if has(b, 0, B):
                    dve.wait_ge(s_sg, b + 1)
                    nc.vector.tensor_tensor(u[:].rearrange("p (t f) -> p t f", t=T), guv[:, :, 1, 0:FH], sg[:], ALU.mult)\
                        .then_inc(s_u, 1)
                    dve.wait_ge(s_u, b + 1)
                    qu.scales(link, u, u[:].rearrange("p (g k) -> p g k", k=16))
                if has(b, 0, B - 1):
                    scale_x(b + 1)
                    rebuild_x(b + 1)
                if has(b, 0, B):
                    wait(dve, s_uT, b)
                    qu.rebuild(dve, link, b, uq[:])
                if has(b, -1, B - 2):
                    stats_of(b + 2)
                if has(b, 0, B):
                    dve.wait_ge(s_y, b + 1)
                    wait(dve, s_x, b)
                    nc.vector.tensor_tensor(yg[:], bankY[:, 0:T * C].rearrange("p (t c) -> p t c", t=T),
                                            rows[:, b, 3 * C:4 * C].unsqueeze(1).to_broadcast([P, T, C]), ALU.mult).then_inc(s_yg, 1)

            def prologue():
                stats_of(0)
                dve.wait_ge(loads["q"], 16 * 5)
                qw1.scales(link, None, m["wraw1"][:].rearrange("p a k (g j) -> p (a k g) j", j=16))
                qw2.scales(link, None, m["wraw2"][:].rearrange("p (g j) -> p g j", j=16))
                normalise(0)
                qw1.rebuild(dve, link, 0, wq[:])
                qw2.rebuild(dve, link, 0, wdq[:])
                stats_of(1)
                scale_x(0)
                rebuild_x(0)

            run(dve, 1, slot, prologue, [link])

        @block.scalar
        def _(act):
            def move_x(b):
                act.wait_ge(s_xT, b + 1)
                wait(act, s_gu, b)
                nc.scalar.copy(hqT[:], bankX[:, 0:T * P].rearrange("p (t q) -> p t q", t=T)).then_inc(s_xTe, 1)

            def silu(b):
                act.wait_ge(s_gu, b + 1)
                wait(act, s_u, b)
                nc.scalar.activation(sg[:], guv[:, :, 0, 0:FH], ACT.Silu).then_inc(s_sg, 1)

            def slot(b, k, par):
                if has(b, 0, B):
                    qu.magnitude(act, b)
                if has(b, 0, B - 1):
                    qx.magnitude(act, b + 1)
                    move_x(b + 1)
                    silu(b + 1)
                if has(b, 0, B):
                    act.wait_ge(s_uT, b + 1)
                    wait(act, s_y, b)
                    for t in range(T):
                        nc.scalar.copy(uT[:, t, 0:2, :], bankU[t][:, 0:2 * P].rearrange("p (c q) -> p c q", c=2))
                        last = nc.scalar.copy(uT[0:96, t, 2, :], bankU[t][0:96, 2 * P:3 * P])
                    last.then_inc(s_uTe, 1)

            def prologue():
                qw1.magnitude(act, 0)
                qw2.magnitude(act, 0)
                act.wait_ge(s_wT, 1)
                for a in range(2):
                    nc.scalar.copy(wguT[:, a, :], bankU[a][:, 0:3 * P])
                nc.scalar.copy(wdT[:, 0:2, :], bankX[:, 0:2 * P].rearrange("p (c q) -> p c q", c=2))
                nc.scalar.copy(wdT[0:96, 2, :], bankX[0:96, 2 * P:3 * P]).then_inc(s_wTe, 1)
                qx.magnitude(act, 0)
                move_x(0)
                silu(0)

            run(act, 1, slot, prologue)

        @block.tensor
        def _(pe):
            def gate_up(b):
                pe.wait_ge(qx.done, b + 1)
                wait(pe, s_xTe, b)
                for t in range(T):
                    last = nc.tensor.transpose(bankX[:, P * t:P * t + P], hq[:, C * t:C * t + C], ident)
                last.then_inc(s_xT, 1)
                pe.wait_ge(s_xTe, b + 1)
                wait(pe, s_u, b)
                for t in range(T):
                    for a in range(2):
                        last = nc.tensor.matmul(guv[:, t, a, 0:FH], hqT[:, t, :], wguT[:, a, 0:FH], start=True, stop=True)
                last.then_inc(s_gu, 1)

            def down(b):
                pe.wait_ge(qu.done, b + 1)
                wait(pe, s_uTe, b)
                for t in range(T):
                    for c, (at, w) in enumerate(FCH):
                        last = nc.tensor.transpose(bankU[t][0:w, P * c:P * c + P], uq[:, FH * t + at:FH * t + at + w], ident)
                last.then_inc(s_uT, 1)
                pe.wait_ge(s_uTe, b + 1)
                wait(pe, s_yg, b)
                for t in range(T):
                    for c, (at, w) in enumerate(FCH):
                        last = nc.tensor.matmul(bankY[:, C * t:C * t + C], uT[0:w, t, c, :], wdT[0:w, c, :], start=c == 0, stop=c == 2)
                last.then_inc(s_y, 1)

            def slot(b, k, par):
                if has(b, 0, B - 1):
                    gate_up(b + 1)
                if has(b, 0, B):
                    down(b)

            def prologue():
                pe.wait_ge(qw1.done, 1)
                pe.wait_ge(qw2.done, 1)
                for a in range(2):
                    for c in range(3):
                        nc.tensor.transpose(bankU[a][:, P * c:P * c + P], wq[:, 3 * C * a + C * c:3 * C * a + C * c + C], ident)
                for c, (at, w) in enumerate(FCH):
                    last = nc.tensor.transpose(bankX[0:w, P * c:P * c + P], wdq[:, at:at + w], ident)
                last.then_inc(s_wT, 1)
                pe.wait_ge(s_wTe, 1)
                gate_up(0)

            run(pe, 1, slot, prologue)


def constants(np):
    k = np.zeros((P, K_END), np.float32)
    row = np.arange(P)[:, None]
    k[:, K_ID:K_ID + 128] = np.eye(P)

    def window(W, t):
        kk = np.arange(2 * W)[None, :]
        i = row % W
        ok = (kk > i) & (kk <= i + W)
        if t == 0:
            ok &= (row // W > 0) | (kk >= W)
        return np.where(ok, 0.0, NEG)

    for t in range(T):
        k[:, K_LOC0 + 64 * t:K_LOC0 + 64 * t + 64] = window(32, t)
        k[:, K_LAT + 64 * t:K_LAT + 64 * t + 64] = np.where(np.arange(64)[None, :] <= (P * t + row) // 4, 0.0, NEG)
        k[:, K_LOC1 + 128 * t:K_LOC1 + 128 * t + 128] = window(64, t)
    q = np.arange(P)[None, :]
    s = np.float32(HD) ** -0.5
    k[:, K_Q0:K_Q0 + 128] = (row // 32 == q // 32) * s
    for g in range(2):
        k[:, K_Q1 + 128 * g:K_Q1 + 128 * g + 128] = ((row // 64 == q // 64) & (row % 64 // 32 == g)) * s
    k[:, K_S:K_S + 4] = row % 32 // 8 == np.arange(4)[None, :]
    k[:, K_GK:K_GK + 8] = (row // 8 == np.arange(8)[None, :]) * 0.25
    k[:, K_H:K_H + 16] = row // 8 == np.arange(16)[None, :]
    k[:, K_TRI:K_TRI + 64] = (np.arange(8)[None, :] < np.arange(8)[:, None]).reshape(1, 64)
    for b in range(B):
        k[b, K_SEL + 128 * b:K_SEL + 128 * b + 128] = 1.0
    return k


_INS = ["L0_attn_x", "L0_attn_wq", "L0_attn_wk", "L0_attn_wv", "L0_attn_wgq", "L0_attn_wgk", "L0_attn_wgv", "L0_attn_r_out_w",
        "L0_attn_gate_local_w", "L0_attn_gate_remote_w", "L0_attn_w_out", "L0_ffn_Wg", "L0_ffn_bg", "L0_ffn_W1", "L0_ffn_b1",
        "L0_ffn_W2", "L0_ffn_b2", "L0_c", "L0_wmod", "L1_attn_Wq", "L1_attn_Wk", "L1_attn_Wv", "L1_attn_Wo", "L1_ffn_w_gate",
        "L1_ffn_w_up", "L1_ffn_w_down", "L1_c", "L1_wmod"]


def kernel(**inputs):
    import numpy as np
    import concourse.bacc as bacc
    from concourse.bass_utils import run_bass_kernel_spmd
    nc = bacc.Bacc("TRN2", target_bir_lowering=False, num_devices=1)
    arrays, io = {}, {}
    for name in _INS:
        a = np.ascontiguousarray(inputs[name])
        arrays[f"in_{name}"] = a
        io[name] = nc.dram_tensor(f"in_{name}", a.shape, mybir.dt.from_np(a.dtype), kind="ExternalInput").ap()
    arrays["constants"] = constants(np)
    io["constants"] = nc.dram_tensor("constants", (P, K_END), F32, kind="ExternalInput").ap()
    out = nc.dram_tensor("out", (B, T * P, C), F32, kind="ExternalOutput").ap()
    build(nc, io, out)
    r = run_bass_kernel_spmd(nc, [arrays], core_ids=[0])
    return r.results[0]["out"]
```

```python
from contextlib import ExitStack

import concourse.bass as bass
from concourse import mybir

ALU = mybir.AluOpType
ACT = mybir.ActivationFunctionType
BF16 = mybir.dt.bfloat16
F32 = mybir.dt.float32
I32 = mybir.dt.int32
AX = mybir.AxisListType.X

P = 128
C = 128
B = 8
T = 2
H = 16
HD = 8
LATH = 8
NLAT = 64
E = 8
HC = 4
FH = 352
FCH = [(0, 128), (128, 128), (256, 96)]
NEG = -1e30
PAD = 64
K_ID = 0
K_LOC0 = K_ID + 128
K_LAT = K_LOC0 + 2 * 64
K_LOC1 = K_LAT + 2 * 64
K_Q0 = K_LOC1 + 2 * 128
K_Q1 = K_Q0 + 128
K_S = K_Q1 + 256
K_GK = K_S + 4
K_H = K_GK + 8
K_TRI = K_H + 16
K_SEL = K_TRI + 64
K_END = K_SEL + 8 * 128


def wait(eng, sem, value):
    if isinstance(value, int) and value <= 0:
        return
    eng.wait_ge(sem, value)


def settle(eng):
    eng.nop(nofuse=True)


class Chain:

    def __init__(self, eng, sem, start=0):
        self.eng, self.sem, self.n, self.it, self.per = eng, sem, start, None, 0

    def __call__(self, ins):
        ins.then_inc(self.sem, 1)
        self.n += 1
        self.eng.wait_ge(self.sem, self.n if self.it is None else self.it * self.per + self.n)

    def enter(self, it, first, per):
        self.it, self.per, self.at = it, per, self.n
        self.n -= first * per

    def leave(self, first, trips):
        took = self.n + first * self.per - self.at
        assert took == self.per, (self.sem, took, self.per)
        self.n = self.at + trips * self.per
        self.it = None


def has(b, lo, hi):
    return not isinstance(b, int) or lo <= b < hi


def run(eng, slots, slot, prologue, chains=(), ahead=1, after=2):
    prologue()
    for b in range(-ahead, 2):
        for k in range(slots):
            slot(b, k, b % 2)
    with eng.Fori(1, B // 2 - 1) as it:
        for c in chains:
            c.enter(it, 1, c.per_pair)
        for par in range(2):
            for k in range(slots):
                slot(2 * it + par, k, par)
    for c in chains:
        c.leave(1, B // 2 - 2)
    for b in range(B - 2, B + after):
        for k in range(slots):
            slot(b, k, b % 2)


def setup(nc, io, m, loads):
    with ExitStack() as ctx:
        def sb(name, shape, dt=F32):
            return ctx.enter_context(nc.sbuf_tensor(name, shape, dt))

        def sem(name):
            return ctx.enter_context(nc.semaphore(name))

        c_sb = sb("c_sb", [B, 2, C])
        c_exp = sb("c_exp", [B, 2, C])
        c_sig = sb("c_sig", [B, 2, C])
        c_silu = sb("c_silu", [B, 2, C])
        cT = sb("cT", [P, 2, B])
        wmod = [sb(f"wmod{i}", [P, 6 * C]) for i in range(2)]
        mod8 = sb("mod8", [B, 2, 6 * C])
        gsgn = sb("gsgn", [B, 2, 2, C])
        gabs = sb("gabs", [B, 2, 2, C])
        wqT0 = sb("wqT0", [P, C])
        gcol = sb("gcol", [P, 2])
        G = sb("G", [P, 2, H])
        wraw = sb("wraw", [P, 4, C])
        b1row = sb("b1row", [E * HC, C])
        ps = [ctx.enter_context(nc.psum_tensor(f"su{i}", [P, 512], F32)) for i in range(8)]
        s_small, s_c, s_wm, s_w0, s_exp, s_pe, s_dve, s_act, s_chain, s_ev, s_pool = [
            sem(n) for n in ["ld_const", "ld_c", "ld_wmod", "ld_w", "c_exp_done", "pe_filled", "dve_done",
                             "act_done", "dve_chain", "bank_empty", "pool_done"]]
        con = m["con"]
        ident = con[:, K_ID:K_ID + 128]
        block = ctx.enter_context(nc.Block())

        @block.sync
        def _(sp):
            sp.dma_start(c_sb[:, 0, :], io["L0_c"]).then_inc(s_c, 16)
            sp.dma_start(c_sb[:, 1, :], io["L1_c"]).then_inc(s_c, 16)
            sp.dma_start(con[:], io["constants"]).then_inc(s_small, 16)
            sp.dma_start(wmod[0][:], io["L0_wmod"]).then_inc(s_wm, 16)
            sp.dma_start(m["x"][:], io["L0_attn_x"].rearrange("b (t p) f -> p (b t) f", p=P)).then_inc(loads["x"], 16)
            sp.dma_start(m["wq0"][:], io["L0_attn_wq"]).then_inc(s_w0, 16)
            sp.dma_start(gcol[:, 0:1], io["L0_attn_gate_local_w"].rearrange("h (d a) -> (h d) a", a=1)).then_inc(s_w0, 16)
            sp.dma_start(gcol[:, 1:2], io["L0_attn_gate_remote_w"].rearrange("h (d a) -> (h d) a", a=1)).then_inc(s_w0, 16)
            sp.dma_start(m["wk0"][:], io["L0_attn_wk"]).then_inc(s_w0, 16)
            sp.dma_start(m["wv0"][:], io["L0_attn_wv"]).then_inc(s_w0, 16)
            sp.dma_start(m["wgq"][:], io["L0_attn_wgq"]).then_inc(s_w0, 16)
            sp.dma_start(m["wgk"][:], io["L0_attn_wgk"]).then_inc(s_w0, 16)
            sp.dma_start(m["wgv"][:], io["L0_attn_wgv"]).then_inc(s_w0, 16)
            sp.dma_start(m["rout"][:], io["L0_attn_r_out_w"]).then_inc(s_w0, 16)
            sp.dma_start(m["wo0"][:], io["L0_attn_w_out"]).then_inc(s_w0, 16)
            sp.dma_start(b1row[:], io["L0_ffn_b1"].rearrange("e (c p) -> (e c) p", p=P)).then_inc(s_w0, 16)
            sp.wait_ge(s_w0, 16 * 15)
            sp.wait_ge(loads["x"], 16)

        @block.scalar
        def _(act):
            act.dma_start(wmod[1][:], io["L1_wmod"]).then_inc(s_wm, 16)
            for i, n in enumerate(["Wq", "Wk", "Wv", "Wo"]):
                act.dma_start(wraw[:, i, :], io["L1_attn_" + n]).then_inc(s_w0, 16)
            act.dma_start(m["w1"][:], io["L0_ffn_W1"].rearrange("e f n -> f e n")).then_inc(loads["ffn"], 16)
            act.dma_start(m["w2"][:], io["L0_ffn_W2"].rearrange("e (c p) f -> p (e c) f", p=P)).then_inc(loads["ffn"], 16)
            act.dma_start(m["wg"][:], io["L0_ffn_Wg"]).then_inc(loads["ffn"], 16)
            act.dma_start(m["bg"][:], io["L0_ffn_bg"].rearrange("(a e) -> a e", a=1)).then_inc(loads["ffn"], 16)
            act.dma_start(m["b2"][:], io["L0_ffn_b2"]).then_inc(loads["ffn"], 16)
            for i, n in enumerate(["w_gate", "w_up"]):
                act.dma_start(m["wraw1"][:, i, 0:2, :], io["L1_ffn_" + n][0:256, :].rearrange("(k p) f -> p k f", p=P)).then_inc(loads["q"], 16)
                act.dma_start(m["wraw1"][0:96, i, 2, :], io["L1_ffn_" + n][256:FH, :]).then_inc(loads["q"], 16)
            act.dma_start(m["wraw2"][:], io["L1_ffn_w_down"]).then_inc(loads["q"], 16)
            act.wait_ge(s_c, 32)
            nc.scalar.activation(c_exp[:], c_sb[:], ACT.Exp, scale=-1.0).then_inc(s_exp, 1)
            for b in range(B):
                act.wait_ge(s_pe, 8 + 2 * b)
                nc.scalar.copy(m["gates0"][:, b, :], ps[2 * (b % 2)][:, 0:256]).then_inc(s_act, 1)
                act.wait_ge(s_pe, 9 + 2 * b)
                nc.scalar.copy(m["rows1"][:, b, :], ps[2 * (b % 2) + 1][:, :]).then_inc(s_act, 1)

        @block.gpsimd
        def _(pool):
            link = Chain(pool, s_pool)
            nc.gpsimd.memset(m["hT"][:], 0.0)
            nc.gpsimd.memset(m["mhalf"][:], -0.5)
            for k in range(2):
                nc.gpsimd.memset(m["V"][k][:], 0.0)
                last = nc.gpsimd.memset(m["GV"][k][:], 0.0)
            link(last)
            link(nc.gpsimd.memset(m["ones"][:], 1.0))
            link(nc.gpsimd.memset(m["wraw1"][96:128, :, 2, :], 0.0))
            for r in range(2):
                for k in range(2):
                    nc.gpsimd.memset(m["V0"][k][64 * r:64 * r + 64, :, :, 9 * r + 8:9 * r + 9], 1.0)
                    last = nc.gpsimd.memset(m["GV"][k][64 * r:64 * r + 64, :, 9 * r + 8:9 * r + 9], 1.0)
                link(last)

        @block.vector
        def _(dve):
            link = Chain(dve, s_chain)
            dve.wait_ge(s_exp, 1)
            link(nc.vector.tensor_scalar_add(c_sig[:], c_exp[:], 1.0))
            link(nc.vector.reciprocal(c_exp[:], c_sig[:]))
            nc.vector.tensor_tensor(c_silu[:], c_sb[:], c_exp[:], ALU.mult).then_inc(s_dve, 1)
            dve.wait_ge(s_pe, 1)
            nc.vector.tensor_copy(cT[:], ps[4][:, 0:2 * B].rearrange("p (l b) -> p l b", l=2)).then_inc(s_dve, 1)
            dve.wait_ge(s_pe, 2)
            for i in range(2):
                link(nc.vector.tensor_copy(m["modT"][:, i], ps[5][:, 48 * i:48 * i + 48].rearrange("p (j b) -> p j b", b=B)))
                link(nc.vector.tensor_scalar_add(m["modT"][:, i, 1:5:3, :], m["modT"][:, i, 1:5:3, :], 1.0))
            dve.wait_ge(s_pe, 3)
            for i in range(2):
                for j in range(2):
                    link(nc.vector.tensor_copy(mod8[:, i, 384 * j:384 * j + 384], ps[6 if j == 0 else 7][0:B, :384] if i == 0 else ps[2 * j][0:B, :384]))
            gate = mod8[:].rearrange("p l (a j c) -> p (l a) j c", a=2, j=3)[:, :, 2, :]
            sg, ab = (t[:].rearrange("p l a c -> p (l a) c") for t in (gsgn, gabs))
            link(nc.vector.tensor_scalar(sg, gate, 0.0, 2.0, ALU.is_ge, ALU.mult))
            link(nc.vector.tensor_scalar_add(sg, sg, -1.0))
            link(nc.vector.tensor_tensor(ab, gate, sg, ALU.mult))
            link(nc.vector.scalar_tensor_tensor(gate, ab, 0.25, sg, ALU.max, ALU.mult))
            nc.vector.tensor_scalar_add(mod8[:, 1, 4 * C:5 * C], mod8[:, 1, 4 * C:5 * C], 1.0).then_inc(s_dve, 1)
            dve.wait_ge(s_small, 16)
            nc.vector.tensor_copy(m["identb"][:], ident)
            nc.vector.tensor_copy(m["maskb"][:], con[:, K_LOC0:K_Q0])
            dve.wait_ge(s_w0, 16 * 15)
            dve.wait_ge(s_pe, 4)
            nc.vector.tensor_copy(wqT0[:], ps[4][:, 0:128])
            for i in range(2):
                last = nc.vector.tensor_scalar(G[:, i, :], con[:, K_H:K_H + H], gcol[:, i:i + 1], None, ALU.mult)
            last.then_inc(s_dve, 1)
            for p in range(4):
                for j in range(4):
                    nc.vector.tensor_copy(m["WqD0"][:, p, j, :], m["wq0"][:, 32 * p:32 * p + 32])
            dve.wait_ge(s_pe, 5)
            nc.vector.tensor_copy(m["WG"][:], ps[5][:, 0:32])
            dve.wait_ge(s_pe, 6)
            for j in range(2):
                nc.vector.tensor_copy(m["WqD1"][:, :, j, :], ps[6][:, 0:128].rearrange("p (g f) -> p g f", g=2))
            nc.vector.tensor_copy(m["w1T"][:], ps[6][:, 128:512].rearrange("p (w f) -> p w f", w=3))
            dve.wait_ge(s_pe, 7)
            nc.vector.tensor_copy(m["b1T"][:], ps[7][:, 0:E * HC]).then_inc(s_dve, 1)
            dve.wait_ge(s_dve, 5)

        @block.tensor
        def _(pe):
            pe.wait_ge(s_small, 16)
            pe.wait_ge(s_dve, 1)
            for i in range(2):
                last = nc.tensor.transpose(ps[4][:, B * i:B * i + B], c_silu[:, i, :], con[0:B, 0:B])
            last.then_inc(s_pe, 1)
            pe.wait_ge(s_dve, 2)
            pe.wait_ge(s_wm, 32)
            for i in range(2):
                for j in range(6):
                    last = nc.tensor.matmul(ps[5][:, 48 * i + B * j:48 * i + B * j + B], wmod[i][:, C * j:C * j + C], cT[:, i, :],
                                            start=True, stop=True)
            last.then_inc(s_pe, 1)
            for i in range(2):
                for j in range(2):
                    bank = ps[6 + j] if i == 0 else ps[2 * j]
                    last = nc.tensor.matmul(bank[0:B, 0:384], cT[:, i, :], wmod[i][:, 384 * j:384 * j + 384], start=True, stop=True)
            last.then_inc(s_pe, 1)
            pe.wait_ge(s_w0, 16 * 15)
            nc.tensor.transpose(ps[4][:, 0:128], m["wq0"][:], ident).then_inc(s_pe, 1)
            pe.wait_ge(s_dve, 4)
            nc.tensor.matmul(ps[5][:, 0:32], wqT0[:], G[:].rearrange("p a h -> p (a h)"), start=True, stop=True).then_inc(s_pe, 1)
            for i in range(4):
                last = nc.tensor.transpose(ps[6][:, 128 * i:128 * i + 128], wraw[:, i, :], ident)
            last.then_inc(s_pe, 1)
            nc.tensor.transpose(ps[7][:, 0:E * HC], b1row[:], con[0:E * HC, 0:E * HC]).then_inc(s_pe, 1)
            for b in range(B):
                pick = con[0:B, K_SEL + 128 * b:K_SEL + 128 * b + 128]
                if b >= 2:
                    pe.wait_ge(s_act, 2 * (b - 1))
                for j in range(2):
                    last = nc.tensor.matmul(ps[2 * (b % 2)][:, 128 * j:128 * j + 128], pick, mod8[:, 0, 384 * j + 256:384 * j + 384],
                                            start=True, stop=True)
                last.then_inc(s_pe, 1)
                nc.tensor.matmul(ps[2 * (b % 2) + 1][:, :], pick, mod8[:, 1, 256:768], start=True, stop=True).then_inc(s_pe, 1)
            pe.wait_ge(s_act, 2 * B)


def attention(nc, m, layer):
    L0 = layer == 0
    W = 32 if L0 else 64
    J = P // W
    KW = 2 * W
    FR = P // J
    NP = C // FR
    NU = 6 if L0 else 8
    NT = NU // T
    scale = float(HD) ** -0.5
    JOBS = ([(0, "V1", 0), (0, "T", 1), (1, "K", 1), (1, "RT", -1), (2, "Q0", 1), (2, "R", -1), (3, "Q1", 1), (3, "GA", 1),
             (4, "V0", 1), (4, "CT", -1), (5, "GB", 1), (5, "Y", -1)] if L0 else
            [(0, "T", 1), (1, "K", 1), (2, "Q0", 1), (3, "CT", -1), (4, "V0", 1), (5, "Y", -1)])
    NAMES = [name for _, name, _ in JOBS]
    GATE = (0, 2) if L0 else (6, 1)
    with ExitStack() as ctx:
        def sb(name, shape, dt=F32):
            return ctx.enter_context(nc.sbuf_tensor(f"a{layer}_{name}", shape, dt))

        def pb(name):
            return ctx.enter_context(nc.psum_tensor(f"a{layer}_{name}", [P, 512], F32))

        def sem(name):
            return ctx.enter_context(nc.semaphore(f"a{layer}_{name}"))

        stats = sb("stats", [P, T, 6])
        mv = sb("mv", [P, T, 2])
        veps = sb("veps", [P, T])
        rstd = sb("rstd", [P, T])
        negmean = sb("negmean", [P, T])
        shift = sb("shift", [P, T])
        xn = sb("xn", [P, T, C])
        Km = [sb(f"Km{k}", [P, NP * T, 4, KW]) for k in range(2)]
        prob = sb("prob", [P, 4, 512])
        nmax = sb("nmax", [P, 2, 8])
        pT = sb("pT", [P, 2, 512])
        Osel = sb("Osel", [P, T, H, 9])
        coef = sb("coef", [P, 2, T, H])
        comb = sb("comb", [P, T, C])
        combT = sb("combT", [P, T, P])
        yg = sb("yg", [P, T, C])
        if L0:
            pair = sb("pair", [P, 2 * NLAT])
            pool4 = sb("pool4", [P, 2, NLAT])
            hT2 = sb("hT2", [P, 8, 2, KW])
            GQT = [sb(f"GQT{k}", [64, T, P]) for k in range(2)]
            GKm = [sb(f"GKm{k}", [64, LATH, NLAT]) for k in range(2)]
            gz = [sb(f"gz{k}", [P, 2, T, H]) for k in range(2)]
            recl = sb("recl", [P, LATH])
            rem = sb("rem", [P, T, 64])
            remT = sb("remT", [64, T, P])
            local = sb("local", [P, T, C])
            remote = sb("remote", [P, T, C])
        hT, Qbd, V, GV, con, identb, modT, x = (m[k] for k in ["hT", "Qbd", "V0" if L0 else "V1", "GV", "con", "identb", "modT", "x"])
        wk, wv = (m["wk0"][:], m["wv0"][:]) if L0 else (m["w1T"][:, 0, :], m["w1T"][:, 1, :])
        wo = m["wo0"][:] if L0 else m["w1T"][:, 2, :]
        WqD = m["WqD0" if L0 else "WqD1"]
        gates_b = m["gates0"] if L0 else m["rows1"]
        ident = con[:, K_ID:K_ID + 128]
        bankS = [pb("S0"), pb("S1")]
        bankT = [pb("T0"), pb("T1")]
        bankO = [pb("O0"), pb("O1")]
        bankJ = [pb("J0"), pb("J1")]
        bank_of = {name: bankJ[i % 2] for i, name in enumerate(NAMES)}
        filled = {name: sem(f"{name}_filled") for name in NAMES}
        read = {name: sem(f"{name}_read") for name in NAMES}
        s_scores, s_shift, s_prob, s_tr, s_pT, s_pv, s_oev = [sem(n) for n in [
            "scores_ready", "shifted", "probs_ready", "probs_transposed", "pT_ready", "pv_done", "O_read"]]
        NOE = NU if L0 else T
        s_mv, s_rstd, s_xn, s_pool4, s_rem, s_comb, s_x, s_loc, s_h2, s_coef = [sem(n) for n in [
            "stats_ready", "rstd_ready", "xn_ready", "pooled_ready", "rem_ready", "comb_ready", "x_updated",
            "local_done", "windows_ready", "coef_ready"]]
        s_ones, s_dch, s_pch = sem("ones_set"), sem("dve_chain"), sem("pool_chain")
        block = ctx.enter_context(nc.Block())

        def jobs(b, k):
            return [(name, b + db) for at, name, db in JOBS if at == k and has(b + db, 0, B)]

        def near(b, k, lag):
            away = (k - lag) // NU
            return NU * b + (k - lag), b + away, (k - lag) % NU, away

        def kind(u):
            return u % NT == 1, (u % NT) // 2

        @block.gpsimd
        def _(pool):
            link = Chain(pool, s_pch)
            link.per_pair = 2 * (2 + L0)

            def rstd_of(b):
                pool.wait_ge(s_mv, b + 1)
                wait(pool, s_xn, b)
                settle(pool)
                nc.gpsimd.tensor_scalar_mul(negmean[:], mv[:, :, 0], -1.0)
                link(nc.gpsimd.tensor_scalar_add(veps[:], mv[:, :, 1], 1e-5))
                link(nc.gpsimd.tensor_tensor(rstd[:], veps[:], m["mhalf"][:, 0:T], ALU.pow))
                nc.gpsimd.tensor_tensor(shift[:], rstd[:], negmean[:], ALU.mult).then_inc(s_rstd, 1)

            def windows_of(b):
                pool.wait_ge(read["T"], b + 1)
                wait(pool, filled["V1"], b)
                settle(pool)
                for half in range(2):
                    at = PAD - W + W * half
                    last = nc.gpsimd.tensor_copy(hT2[:, :, :, W * half:W * half + W],
                                                 hT[:, at:at + T * P].rearrange("p (w k) -> p w k", k=W).unsqueeze(2)
                                                 .to_broadcast([P, 8, 2, W]))
                last.then_inc(s_h2, 1)

            def pool_of(b):
                h2 = hT[:, PAD:PAD + T * P].rearrange("p (n c) -> p n c", c=2)
                link(nc.gpsimd.tensor_tensor(pair[:], h2[:, :, 0], h2[:, :, 1], ALU.add))
                wait(pool, filled["GB"], b)
                p2 = pair[:].rearrange("p (n c) -> p n c", c=2)
                for i in range(2):
                    last = nc.gpsimd.tensor_tensor(pool4[:, i, :], p2[:, :, 0], p2[:, :, 1], ALU.add)
                last.then_inc(s_pool4, 1)

            def slot(b, k, par):
                if k == 0 and has(b + 1, 0, B):
                    rstd_of(b + 1)
                if L0 and k == 1 and has(b + 1, 0, B):
                    windows_of(b + 1)
                    pool_of(b + 1)
                if L0 and k == 3 and has(b - 1, 0, B):
                    pool.wait_ge(s_coef, b)
                    wait(pool, s_comb, b - 1)
                    nc.gpsimd.tensor_tensor(local[:].rearrange("p t (h d) -> p (t h) d", d=HD),
                                            Osel[:, :, :, 0:8].rearrange("p t h d -> p (t h) d"),
                                            coef[:, 0].rearrange("p t h -> p (t h)").unsqueeze(2).to_broadcast([P, T * H, HD]),
                                            ALU.mult).then_inc(s_loc, 1)
                    pool.wait_ge(s_loc, b)
                    pool.wait_ge(read["R"], b)
                    wait(pool, filled["CT"], b - 1)
                    nc.gpsimd.tensor_tensor(comb[:], local[:], remote[:], ALU.add).then_inc(s_comb, 1)
                if k == GATE[0] and has(b - GATE[1], 0, B):
                    gb = b - GATE[1]
                    pool.wait_ge(read["Y"], gb + 1)
                    xt = x[:, bass.ds(T * gb, T), :]
                    nc.gpsimd.tensor_tensor(xt, xt, yg[:], ALU.add).then_inc(s_x, 1)

            def prologue():
                if not L0:
                    for k in range(2):
                        last = nc.gpsimd.memset(m["V"][k][:], 1.0)
                    last.then_inc(s_ones, 1)

            run(pool, NU, slot, prologue, [link])

        @block.vector
        def _(dve):
            link = Chain(dve, s_dch)
            link.per_pair = 2 * (NU + 1 + (NT if L0 else 1))

            def stats_of(b):
                wait(dve, s_rstd, b)
                for t in range(T):
                    last = nc.vector.bn_stats(stats[:, t, :], x[:, T * b + t, :])
                link(last)
                settle(dve)
                for t in range(T):
                    last = nc.vector.bn_aggr(mv[:, t, :], stats[:, t, :])
                last.then_inc(s_mv, 1)

            def spread_q(b, par, name):
                bank = bank_of[name]
                dve.wait_ge(filled[name], b + 1)
                for v in range(2 if L0 else 4):
                    var = 2 * int(name[1]) + v
                    src = bank[:, 256 * v:256 * v + 256] if L0 else bank[:, 256 * (v // 2):256 * (v // 2) + 256]
                    mask = con[:, K_Q0:K_Q0 + 128] if L0 else con[:, K_Q1 + 128 * (v % 2):K_Q1 + 128 * (v % 2) + 128]
                    last = nc.vector.tensor_tensor(Qbd[par][:, var, :, :], src.rearrange("p (t q) -> p t q", t=T),
                                                   mask.unsqueeze(1).to_broadcast([P, T, P]), ALU.mult)
                last.then_inc(read[name], 1)

            def latents(b, par):
                bank = bank_of["GB"]
                dve.wait_ge(filled["GB"], b + 1)
                nc.vector.tensor_tensor(GKm[par][:], bank[0:64, 0:NLAT].unsqueeze(1).to_broadcast([64, LATH, NLAT]),
                                        con[0:64, K_GK:K_GK + LATH].unsqueeze(2).to_broadcast([64, LATH, NLAT]), ALU.mult)
                for r in range(2):
                    last = nc.vector.tensor_scalar(
                        GV[par][64 * r:64 * r + 64, :, 9 * r:9 * r + 8],
                        bank[64 * r:64 * r + 64, 64:128].rearrange("p (a r d) -> p a r d", r=2, d=HD)[:, :, r, :],
                        0.25, None, ALU.mult)
                last.then_inc(read["GB"], 1)

            def softmax_shift(n, u, slot_of):
                heads = 8 if L0 else 4
                dve.wait_ge(s_scores, n + 1)
                s3 = bankS[u % 2][:].rearrange("p (h k) -> p h k", h=heads)
                mx = nmax[:, u % 2, 0:heads]
                link(nc.vector.tensor_reduce(mx, s3, AX, ALU.max))
                wait(dve, s_tr, n - 3)
                nc.vector.tensor_tensor(prob[:, slot_of, :].rearrange("p (h k) -> p h k", h=heads), s3,
                                        mx.unsqueeze(2).to_broadcast([P, heads, 512 // heads]), ALU.subtract).then_inc(s_shift, 1)

            def read_o(n, b, u):
                t = u // NT
                if not L0:
                    if u % NT != NT - 1:
                        return
                    dve.wait_ge(s_pv, n + 1)
                    for j in range(J):
                        o = bankO[t][W * j:W * j + W, 0:H * 18].rearrange("p (h j e) -> p h j e", j=J, e=9)[:, :, j, :]
                        last = nc.vector.tensor_copy(Osel[W * j:W * j + W, t, :, :], o)
                    last.then_inc(s_oev, 1)
                    return
                lat, g = kind(u)
                dve.wait_ge(s_pv, n + 1)
                if lat:
                    o = bankO[u % 2][:, 0:72].rearrange("p (h e) -> p h e", e=9)
                    link(nc.vector.reciprocal(recl[:], o[:, :, 8]))
                    wait(dve, filled["RT"], b)
                    nc.vector.tensor_tensor(rem[:, t, :].rearrange("p (h d) -> p h d", d=HD), o[:, :, 0:8],
                                            recl[:].unsqueeze(2).to_broadcast([P, LATH, HD]), ALU.mult).then_inc(s_oev, 1)
                    return
                wait(dve, s_loc, b)
                for j in range(J):
                    o = bankO[u % 2][W * j:W * j + W, 0:288].rearrange("p (a j e) -> p a j e", j=J, e=18)[:, :, j, :]
                    dst = Osel[W * j:W * j + W, t, 8 * g:8 * g + 8, :].rearrange("p (a r) e -> p a (r e)", r=2)
                    last = nc.vector.tensor_copy(dst, o)
                last.then_inc(s_oev, 1)

            def combine(b, par):
                dve.wait_ge(s_oev, NOE * (b + 1))
                if not L0:
                    link(nc.vector.reciprocal(coef[:, 0], Osel[:, :, :, 8]))
                    nc.vector.tensor_tensor(comb[:].rearrange("p t (h d) -> p (t h) d", d=HD),
                                            Osel[:, :, :, 0:8].rearrange("p t h d -> p (t h) d"),
                                            coef[:, 0].rearrange("p t h -> p (t h)").unsqueeze(2).to_broadcast([P, T * H, HD]),
                                            ALU.mult).then_inc(s_comb, 1)
                    return
                dve.wait_ge(read["GA"], b + 1)
                wait(dve, s_loc, b)
                nc.vector.scalar_tensor_tensor(coef[:, 0], gz[par][:, 0], 1.0, Osel[:, :, :, 8], ALU.add, ALU.mult)
                link(nc.vector.tensor_scalar_add(coef[:, 1], gz[par][:, 1], 1.0))
                nc.vector.reciprocal(coef[:], coef[:]).then_inc(s_coef, 1)

            def scale_remote(b):
                dve.wait_ge(s_coef, b + 1)
                dve.wait_ge(filled["R"], b + 1)
                wait(dve, s_comb, b)
                nc.vector.tensor_tensor(remote[:].rearrange("p t (h d) -> p t h d", d=HD),
                                        bank_of["R"][:, 0:256].rearrange("p (t h d) -> p t h d", t=T, d=HD),
                                        coef[:, 1].unsqueeze(3).to_broadcast([P, T, H, HD]), ALU.mult).then_inc(read["R"], 1)

            def gate_y(b):
                dve.wait_ge(filled["Y"], b + 1)
                wait(dve, s_x, b)
                nc.vector.tensor_tensor(yg[:], bank_of["Y"][:, 0:256].rearrange("p (t c) -> p t c", t=T),
                                        gates_b[:, b, 0:C].unsqueeze(1).to_broadcast([P, T, C]), ALU.mult).then_inc(read["Y"], 1)

            def slot(b, k, par):
                if k == GATE[0] and has(b - GATE[1], 0, B):
                    gate_y(b - GATE[1])
                n, ub, u, _ = near(b, k, 0)
                if has(ub, 0, B):
                    softmax_shift(n, u, (NU * par + u) % 4)
                if k == 2 and has(b - 1, 0, B):
                    combine(b - 1, 1 - par)
                if L0 and k == 3 and has(b - 1, 0, B):
                    scale_remote(b - 1)
                n2, ub2, u2, _ = near(b, k, 2)
                if has(ub2, 0, B):
                    read_o(n2, ub2, u2)
                for name, jb in jobs(b, k):
                    if name in ("Q0", "Q1"):
                        spread_q(jb, 1 - par, name)
                    if name == "GB":
                        latents(jb, 1 - par)
                if k == 3 and has(b + 2, 0, B) and has(b, -1, B - 2):
                    stats_of(b + 2)

            def prologue():
                dve.wait_ge(m["ld_x"], 16)
                stats_of(0)

            run(dve, NU, slot, prologue, [link])

        @block.scalar
        def _(act):
            def normalise(b):
                act.wait_ge(s_rstd, b + 1)
                wait(act, filled["T"], b)
                for t in range(T):
                    last = nc.scalar.activation(xn[:, t, :], x[:, T * b + t, :], ACT.Identity, bias=shift[:, t:t + 1],
                                                scale=rstd[:, t:t + 1])
                last.then_inc(s_xn, 1)

            def evacuate(b, par, name):
                bank = bank_of[name]
                act.wait_ge(filled[name], b + 1)
                if name == "T":
                    if L0:
                        wait(act, s_pool4, b)
                    last = nc.scalar.activation(hT[:, PAD:PAD + T * P], bank[:, 0:T * P], ACT.Identity,
                                                bias=modT[:, layer, 0, bass.ds(b, 1)], scale=modT[:, layer, 1, bass.ds(b, 1)])
                elif name == "K":
                    for s in range(4):
                        last = nc.scalar.activation(Km[par][:, :, s, :], bank[:].rearrange("p (g k) -> p g k", k=KW), ACT.Copy,
                                                    scale=con[:, K_S + s:K_S + s + 1])
                elif name[0] == "V" and L0:
                    half = int(name[1])
                    for r in range(2):
                        last = nc.scalar.copy(
                            V[par][64 * r:64 * r + 64, 4 * half:4 * half + 4, :, 9 * r:9 * r + 8],
                            bank[64 * r:64 * r + 64, :].rearrange("p (w a r d) -> p w a r d", w=4, r=2, d=HD)[:, :, :, r, :])
                elif name == "V0":
                    last = nc.scalar.copy(V[par].rearrange("p w h e -> p (w h) e")[:, :, 0:8],
                                          bank[:].rearrange("p (g d) -> p g d", d=HD))
                elif name == "GA":
                    nc.scalar.activation(GQT[par][:], bank[0:64, 0:256].rearrange("p (t q) -> p t q", t=T), ACT.Copy, scale=scale)
                    wait(act, s_coef, b - 1)
                    last = nc.scalar.activation(gz[par][:], bank[:, 256:320].rearrange("p (t a h) -> p a t h", t=T, a=2), ACT.Exp,
                                                scale=-1.0)
                elif name == "RT":
                    last = nc.scalar.copy(remT[:], bank[0:64, 0:256].rearrange("p (t q) -> p t q", t=T))
                elif name == "CT":
                    last = nc.scalar.copy(combT[:], bank[:, 0:256].rearrange("p (t q) -> p t q", t=T))
                last.then_inc(read[name], 1)

            def slot(b, k, par):
                if k == 0 and has(b + 1, 0, B):
                    normalise(b + 1)
                n1, ub1, u1, _ = near(b, k, 1)
                if has(ub1, 0, B):
                    act.wait_ge(s_tr, n1 + 1)
                    wait(act, s_pv, n1 - 1)
                    nc.scalar.copy(pT[:, u1 % 2, :], bankT[u1 % 2][:]).then_inc(s_pT, 1)
                if has(b, 0, B):
                    n, _, u, _ = near(b, k, 0)
                    r = (NU * par + u) % 4
                    act.wait_ge(s_shift, n + 1)
                    nc.scalar.activation(prob[:, r, :], prob[:, r, :], ACT.Exp).then_inc(s_prob, 1)
                for at, name, db in JOBS:
                    if at == k and has(b + db, 0, B) and name not in ("Q0", "Q1", "GB", "R", "Y"):
                        evacuate(b + db, (par + db) % 2, name)

            def prologue():
                if not L0:
                    act.wait_ge(s_ones, 1)

            run(act, NU, slot, prologue)

        @block.tensor
        def _(pe):
            def bank_free(b, i):
                if not isinstance(b, int):
                    q = (i - 2) % len(JOBS)
                    _, name, db = JOBS[q]
                    pe.wait_ge(read[name], b + db + (1 if q < i else 0))
                    return
                for q in range(i % 2, len(JOBS), 2):
                    _, name, db = JOBS[q]
                    if q != i:
                        wait(pe, read[name], max(0, min(B, b + db + (1 if q < i else 0))))

            def job(b, name):
                bank = bank_of[name]
                if name == "T":
                    pe.wait_ge(s_xn, b + 1)
                    for t in range(T):
                        last = nc.tensor.transpose(bank[:, P * t:P * t + P], xn[:, t, :], ident)
                elif name == "K":
                    pe.wait_ge(read["T"], b + 1)
                    for p in range(NP):
                        for j in range(J):
                            at = PAD + W * (j - 1)
                            rhs = hT[:, at:at + T * P].rearrange("p (t q) -> p t q", t=T)[:, :, 0:KW]
                            last = nc.tensor.matmul(bank[FR * j:FR * j + FR, T * KW * p:T * KW * (p + 1)],
                                                    wk[:, FR * p:FR * p + FR], rhs, start=True, stop=True)
                elif name[0] == "Q":
                    for v in range(2):
                        p = 2 * int(name[1]) + v
                        last = nc.tensor.matmul(bank[:, 256 * v:256 * v + 256], WqD[:, p, :, :].rearrange("p j f -> p (j f)"),
                                                hT[:, PAD:PAD + T * P], start=True, stop=True)
                elif name[0] == "V":
                    if L0:
                        pe.wait_ge(s_h2, b + 1)
                    for w in range(4):
                        win = 4 * int(name[1]) + w
                        at = PAD + W * (win - 1)
                        lhsT = hT2[:, win].rearrange("p r k -> p (r k)") if L0 else hT[:, at:at + KW]
                        last = nc.tensor.matmul(bank[:, C * w:C * w + C], lhsT, wv, start=True, stop=True)
                elif name == "GB":
                    pe.wait_ge(s_pool4, b + 1)
                    nc.tensor.matmul(bank[0:64, 0:NLAT], m["wgk"][:], pool4[:, 0, :], start=True, stop=True)
                    last = nc.tensor.matmul(bank[:, 64:128], pool4[:].rearrange("p a n -> p (a n)"), m["wgv"][:],
                                            start=True, stop=True)
                elif name == "GA":
                    nc.tensor.matmul(bank[0:64, 0:256], m["wgq"][:], hT[:, PAD:PAD + T * P], start=True, stop=True)
                    for t in range(T):
                        last = nc.tensor.matmul(bank[:, 256 + 32 * t:288 + 32 * t], hT[:, PAD + P * t:PAD + P * t + P], m["WG"][:],
                                                start=True, stop=True)
                elif name == "RT":
                    pe.wait_ge(s_oev, NU * (b + 1) - 1)
                    settle(pe)
                    for t in range(T):
                        last = nc.tensor.transpose(bank[0:64, P * t:P * t + P], rem[:, t, :], ident)
                elif name == "R":
                    pe.wait_ge(read["RT"], b + 1)
                    for t in range(T):
                        last = nc.tensor.matmul(bank[:, C * t:C * t + C], remT[:, t, :], m["rout"][:], start=True, stop=True)
                elif name == "CT":
                    pe.wait_ge(s_comb, b + 1)
                    for t in range(T):
                        last = nc.tensor.transpose(bank[:, P * t:P * t + P], comb[:, t, :], ident)
                else:
                    pe.wait_ge(read["CT"], b + 1)
                    for t in range(T):
                        last = nc.tensor.matmul(bank[:, C * t:C * t + C], combT[:, t, :], wo, start=True, stop=True)
                last.then_inc(filled[name], 1)

            def scores(n, b, u, par):
                t = u // NT
                lat, g = kind(u) if L0 else (False, u % NT)
                if u == 0:
                    for name in ("K", "Q0", "Q1") if L0 else ("K", "Q0"):
                        pe.wait_ge(read[name], b + 1)
                if lat and t == 0:
                    pe.wait_ge(read["GA"], b + 1)
                    pe.wait_ge(read["GB"], b + 1)
                wait(pe, s_shift, n - 1)
                bank = bankS[u % 2]
                if lat:
                    mask = m["maskb"][:, 128 + 64 * t:192 + 64 * t].unsqueeze(1).to_broadcast([P, LATH, NLAT])
                elif L0:
                    mask = m["maskb"][:, 64 * t:64 * t + 64].unsqueeze(1).to_broadcast([P, 4, KW])
                else:
                    mask = m["maskb"][:, 256 + 128 * t:384 + 128 * t].unsqueeze(1).to_broadcast([P, 4, KW])
                if not L0 or lat:
                    nc.tensor.matmul(bank[:], identb[:], mask, start=True, stop=False)
                if lat:
                    last = nc.tensor.matmul(bank[:], GQT[par][:, t, :], GKm[par][:].rearrange("p h n -> p (h n)"), start=False, stop=True)
                elif L0:
                    for i in range(2):
                        p = 2 * g + i
                        nc.tensor.matmul(bank[:, 256 * i:256 * i + 256], identb[:], mask, start=True, stop=False)
                        last = nc.tensor.matmul(bank[:, 256 * i:256 * i + 256], Qbd[par][:, p, t, :],
                                                Km[par][:, T * p + t, :, :].rearrange("p s k -> p (s k)"), start=False, stop=True)
                else:
                    last = nc.tensor.matmul(bank[:], Qbd[par][:, g, t, :],
                                            Km[par][:, T * (g // 2) + t, :, :].rearrange("p s k -> p (s k)"), start=False, stop=True)
                last.then_inc(s_scores, 1)

            def turn(n, u, r):
                pe.wait_ge(s_prob, n + 1)
                wait(pe, s_pT, n - 1)
                for i in range(4):
                    last = nc.tensor.transpose(bankT[u % 2][:, P * i:P * i + P], prob[:, r, P * i:P * i + P], ident)
                last.then_inc(s_tr, 1)

            def values(n, b, u, par):
                t = u // NT
                lat, g = kind(u) if L0 else (False, u % NT)
                pe.wait_ge(s_pT, n + 1)
                if u == 0:
                    pe.wait_ge(read["V0"], b + 1)
                if L0 and u == NT:
                    pe.wait_ge(read["V1"], b + 1)
                if L0:
                    wait(pe, s_oev, n - 1)
                elif g == 0:
                    wait(pe, s_oev, T * b + t - 1)
                for i in range(4):
                    lhsT = pT[:, u % 2, P * i:P * i + P]
                    if lat:
                        out, rhs = bankO[u % 2][:, 18 * i:18 * i + 18], GV[par][:, i, :]
                    elif L0:
                        out, rhs = bankO[u % 2][:, 72 * i:72 * i + 72], V[par][:, 4 * t:4 * t + 4, 4 * g + i, :]
                    else:
                        h = 4 * g + i
                        out, rhs = bankO[t][:, 18 * h:18 * h + 18], V[par][:, 2 * t:2 * t + 2, h, :]
                    last = nc.tensor.matmul(out, lhsT, rhs, start=True, stop=True)
                last.then_inc(s_pv, 1)

            def slot(b, k, par):
                todo = [(i, name, b + db) for i, (at, name, db) in enumerate(JOBS) if at == k]
                n1, ub1, u1, away1 = near(b, k, 1)
                if has(ub1, 0, B):
                    turn(n1, u1, (NU * ((par + away1) % 2) + u1) % 4)
                nn, ubn, un, awayn = near(b, k, -1)
                for step in range(2):
                    for i, name, jb in todo[step:step + 1]:
                        if has(jb, 0, B):
                            bank_free(b, i)
                            job(jb, name)
                    if step == 0 and has(ubn, 0, B):
                        scores(nn, ubn, un, (par + awayn) % 2)
                n2, ub2, u2, away2 = near(b, k, 2)
                if has(ub2, 0, B):
                    values(n2, ub2, u2, (par + away2) % 2)

            run(pe, NU, slot, lambda: None)


def build(nc, io, out):
    with ExitStack() as ctx:
        def sb(name, shape, dt=F32):
            return ctx.enter_context(nc.sbuf_tensor(name, shape, dt))

        m = {
            "con": sb("con", [P, K_END]), "identb": sb("identb", [P, P], BF16), "maskb": sb("maskb", [P, K_Q0 - K_LOC0], BF16),
            "x": sb("x", [P, B * T, C]), "modT": sb("modT", [P, 2, 6, B]),
            "gates0": sb("gates0", [P, B, 2 * C]), "rows1": sb("rows1", [P, B, 4 * C]),
            "wq0": sb("wq0", [P, C]), "wk0": sb("wk0", [P, C]), "wv0": sb("wv0", [P, C]), "wo0": sb("wo0", [P, C]),
            "wgq": sb("wgq", [P, 64]), "wgk": sb("wgk", [P, 64]), "wgv": sb("wgv", [P, 64]), "rout": sb("rout", [64, C]),
            "WG": sb("WG", [P, 32]), "WqD0": sb("WqD0", [P, 4, 4, 32]), "WqD1": sb("WqD1", [P, 2, 2, 64]),
            "w1T": sb("w1T", [P, 3, C]), "b1T": sb("b1T", [P, E * HC]),
            "w1": sb("w1", [P, E, HC * P]), "w2": sb("w2", [P, E * HC, C]), "wg": sb("wg", [P, E]), "bg": sb("bg", [1, E]),
            "b2": sb("b2", [E, C]), "wraw1": sb("wraw1", [P, 2, 3, C]), "wraw2": sb("wraw2", [P, FH]),
            "hT": sb("hT", [P, PAD + T * P + PAD]), "ones": sb("ones", [1, P]), "mhalf": sb("mhalf", [P, 2]),
            "Qbd": [sb(f"Qbd{k}", [P, 4, T, P]) for k in range(2)],
            "V": [sb(f"V{k}", [P, 8 * 8 * 18]) for k in range(2)],
            "GV": [sb(f"GV{k}", [P, 4, 18]) for k in range(2)],
        }
        m["V0"] = [v[:].rearrange("p (w a e) -> p w a e", w=8, e=18) for v in m["V"]]
        m["V1"] = [v[:, 0:4 * H * 9].rearrange("p (w h e) -> p w h e", w=4, e=9) for v in m["V"]]
        loads = {k: ctx.enter_context(nc.semaphore(f"ld_{k}")) for k in ["x", "ffn", "q"]}
        m["ld_x"] = loads["x"]
        setup(nc, io, m, loads)
        attention(nc, m, 0)
        experts(nc, m, loads)
        attention(nc, m, 1)
        quant_ffn(nc, m, loads, out)


def experts(nc, m, loads):
    with ExitStack() as ctx:
        def sb(name, shape, dt=F32):
            return ctx.enter_context(nc.sbuf_tensor(f"e_{name}", shape, dt))

        def pb(name):
            return ctx.enter_context(nc.psum_tensor(f"e_{name}", [P, 512], F32))

        def sem(name):
            return ctx.enter_context(nc.semaphore(f"e_{name}"))

        stats, mv, veps, rstd = sb("stats", [P, T, 6]), sb("mv", [P, T, 2]), sb("veps", [P, T]), sb("rstd", [P, T])
        xn = sb("xn", [P, T, C])
        hTe = [sb(f"hT{k}", [P, T * P]) for k in range(2)]
        hid = [sb(f"hid{k}", [P, HC, T * P]) for k in range(2)]
        acc = [sb(f"acc{k}", [P, T, C]) for k in range(2)]
        sel = [sb(f"sel{k}", [P, T, E]) for k in range(2)]
        b2s = sb("b2s", [P, T, C])
        selT = sb("selT", [E, T * P])
        yg = sb("yg", [P, T, C])
        top, lg, ex, tot = sb("top", [P, T]), sb("lg", [P, T, E]), sb("ex", [P, T, E]), sb("tot", [P, T])
        prb, gt, eq, rank = sb("prb", [P, T, E]), sb("gt", [P, T, E, E]), sb("eq", [P, T, E, E]), sb("rank", [P, T, E])
        bankH = [pb(f"H{c}") for c in range(HC)]
        bankY = [pb("Y0"), pb("Y1")]
        bankF = pb("F")
        x, con, modT = m["x"], m["con"], m["modT"]
        ident = con[:, K_ID:K_ID + 128]
        s_hid, s_gelu, s_y, s_acc, s_ff, s_fe, s_mv, s_rstd, s_xn, s_lg, s_ex, s_sel, s_x, s_dch, s_pch = [sem(n) for n in [
            "hidden_ready", "gelu_done", "y_ready", "accumulated", "front_filled", "front_read", "stats_ready", "rstd_ready",
            "xn_ready", "logits_ready", "exp_ready", "weights_ready", "x_updated", "dve_chain", "pool_chain"]]
        NF = 4
        fronts = [(1, "T"), (2, "G"), (5, "ST"), (6, "B2")]
        job = {name: i for i, (_, name) in enumerate(fronts)}
        block = ctx.enter_context(nc.Block())

        @block.gpsimd
        def _(pool):
            link = Chain(pool, s_pch)
            link.per_pair = 4

            def rstd_of(b):
                pool.wait_ge(s_mv, b + 1)
                settle(pool)
                link(nc.gpsimd.tensor_scalar_add(veps[:], mv[:, :, 1], 1e-5))
                nc.gpsimd.tensor_tensor(rstd[:], veps[:], m["mhalf"][:, 0:T], ALU.pow).then_inc(s_rstd, 1)

            def update(b, par):
                pool.wait_ge(s_acc, E * (b + 1))
                wait(pool, s_x, b)
                link(nc.gpsimd.tensor_tensor(yg[:], acc[par][:], m["gates0"][:, b, C:2 * C].unsqueeze(1).to_broadcast([P, T, C]),
                                             ALU.mult))
                xt = x[:, bass.ds(T * b, T), :]
                nc.gpsimd.tensor_tensor(xt, xt, yg[:], ALU.add).then_inc(s_x, 1)

            def slot(b, k, par):
                if k == 0 and has(b, 1, B + 1):
                    update(b - 1, 1 - par)
                if k == 7 and has(b, -1, B - 2):
                    rstd_of(b + 2)

            def prologue():
                rstd_of(0)
                rstd_of(1)

            run(pool, E, slot, prologue, [link], 0, 1)

        @block.vector
        def _(dve):
            link = Chain(dve, s_dch)
            link.per_pair = 2 * 13

            def stats_of(b):
                wait(dve, s_xn, b)
                for t in range(T):
                    last = nc.vector.bn_stats(stats[:, t, :], x[:, T * b + t, :])
                link(last)
                settle(dve)
                for t in range(T):
                    last = nc.vector.bn_aggr(mv[:, t, :], stats[:, t, :])
                last.then_inc(s_mv, 1)

            def normalise(b):
                dve.wait_ge(s_rstd, b + 1)
                wait(dve, s_ff, NF * (b - 1) + 1)
                for t in range(T):
                    last = nc.vector.tensor_scalar(xn[:, t, :], x[:, T * b + t, :], mv[:, t, 0:1], rstd[:, t:t + 1],
                                                   ALU.subtract, ALU.mult)
                last.then_inc(s_xn, 1)

            def logits(b):
                dve.wait_ge(s_ff, NF * b + job["G"] + 1)
                l3 = bankF[:, 0:T * E].rearrange("p (t e) -> p t e", t=T)
                link(nc.vector.tensor_reduce(top[:], l3, AX, ALU.max))
                nc.vector.tensor_tensor(lg[:], l3, top[:].unsqueeze(2).to_broadcast([P, T, E]), ALU.subtract).then_inc(s_fe, 1)

            def select(b, par):
                dve.wait_ge(s_ex, b + 1)
                link(nc.vector.tensor_reduce(tot[:], ex[:], AX, ALU.add))
                link(nc.vector.reciprocal(tot[:], tot[:]))
                link(nc.vector.tensor_tensor(prb[:], ex[:], tot[:].unsqueeze(2).to_broadcast([P, T, E]), ALU.mult))
                other = prb[:].unsqueeze(2).to_broadcast([P, T, E, E])
                own = prb[:].unsqueeze(3).to_broadcast([P, T, E, E])
                nc.vector.tensor_tensor(gt[:], other, own, ALU.is_gt)
                link(nc.vector.tensor_tensor(eq[:], other, own, ALU.is_equal))
                flat = [P, T, E * E]
                gt2, eq2 = (a[:].rearrange("p t e f -> p t (e f)") for a in (gt, eq))
                link(nc.vector.tensor_tensor(eq2, eq2, con[:, K_TRI:K_TRI + E * E].unsqueeze(1).to_broadcast(flat), ALU.mult))
                link(nc.vector.tensor_tensor(gt2, gt2, eq2, ALU.add))
                link(nc.vector.tensor_reduce(rank[:], gt[:], AX, ALU.add))
                link(nc.vector.scalar_tensor_tensor(prb[:], rank[:], 1.5, prb[:], ALU.is_lt, ALU.mult))
                link(nc.vector.tensor_reduce(tot[:], prb[:], AX, ALU.add))
                link(nc.vector.tensor_scalar_add(tot[:], tot[:], 1e-8))
                link(nc.vector.reciprocal(tot[:], tot[:]))
                nc.vector.tensor_tensor(sel[par][:], prb[:], tot[:].unsqueeze(2).to_broadcast([P, T, E]), ALU.mult).then_inc(s_sel, 1)

            def accumulate(n, b, e, par):
                dve.wait_ge(s_y, n + 1)
                if e == 0:
                    dve.wait_ge(s_fe, NF * (b + 1))
                    wait(dve, s_x, b - 1)
                else:
                    wait(dve, s_acc, n)
                for t in range(T):
                    last = nc.vector.scalar_tensor_tensor(acc[par][:, t, :], bankY[e % 2][:, C * t:C * t + C], sel[par][:, t, e:e + 1],
                                                          b2s[:, t, :] if e == 0 else acc[par][:, t, :], ALU.mult, ALU.add)
                last.then_inc(s_acc, 1)

            def slot(b, k, par):
                if has(b, 0, B - 1):
                    if k == 3:
                        logits(b + 1)
                    if k == 4:
                        select(b + 1, 1 - par)
                if has(b, 0, B):
                    accumulate(E * b + k, b, k, par)
                if k == 0 and has(b, 0, B - 1):
                    normalise(b + 1)
                if k == 6 and has(b, -1, B - 2):
                    stats_of(b + 2)

            def prologue():
                stats_of(0)
                normalise(0)
                logits(0)
                select(0, 0)
                stats_of(1)

            run(dve, E, slot, prologue, [link], 0, 1)

        @block.scalar
        def _(act):
            def feed_h(b, par):
                act.wait_ge(s_ff, NF * b + 1)
                nc.scalar.activation(hTe[par][:], bankF[:, 0:T * P], ACT.Identity,
                                     bias=modT[:, 0, 3, bass.ds(b, 1)], scale=modT[:, 0, 4, bass.ds(b, 1)]).then_inc(s_fe, 1)

            def gelu(n, e, par):
                wait(act, s_y, n - 1)
                for c in range(HC):
                    act.wait_ge(s_hid, HC * n + c + 1)
                    nc.scalar.activation(hid[e % 2][:, c, :], bankH[c][:, 0:T * P], ACT.Gelu_apprx_tanh,
                                         bias=m["b1T"][:, HC * e + c:HC * e + c + 1]).then_inc(s_gelu, 1)

            def fronts_of(b, k, par):
                if k == 1:
                    feed_h(b, par)
                if k == 3:
                    act.wait_ge(s_fe, NF * b + job["G"] + 1)
                    wait(act, s_sel, b)
                    nc.scalar.activation(ex[:], lg[:], ACT.Exp).then_inc(s_ex, 1)
                if k == 5:
                    act.wait_ge(s_ff, NF * b + job["ST"] + 1)
                    nc.scalar.copy(selT[:], bankF[0:E, 0:T * P]).then_inc(s_fe, 1)
                if k == 6:
                    act.wait_ge(s_ff, NF * b + job["B2"] + 1)
                    wait(act, s_acc, E * (b - 1) + 1)
                    nc.scalar.copy(b2s[:], bankF[:, 0:T * C].rearrange("p (t c) -> p t c", t=T)).then_inc(s_fe, 1)

            def slot(b, k, par):
                e, nb = (k + 1) % E, b + (k + 1) // E
                if has(nb, 0, B):
                    gelu(E * b + k + 1, e, par)
                if has(b, 0, B - 1):
                    fronts_of(b + 1, k, 1 - par)

            def prologue():
                for k in (1, 3, 5, 6):
                    fronts_of(0, k, 0)
                gelu(0, 0, 0)

            run(act, E, slot, prologue, ahead=0, after=1)

        @block.tensor
        def _(pe):
            def front(b, par, name):
                i = job[name]
                wait(pe, s_fe, NF * b + i)
                if name == "T":
                    pe.wait_ge(s_xn, b + 1)
                    for t in range(T):
                        last = nc.tensor.transpose(bankF[:, P * t:P * t + P], xn[:, t, :], ident)
                elif name == "G":
                    for t in range(T):
                        out = bankF[:, E * t:E * t + E]
                        nc.tensor.matmul(out, hTe[par][:, P * t:P * t + P], m["wg"][:], start=True, stop=False)
                        last = nc.tensor.matmul(out, m["ones"][:], m["bg"][:], start=False, stop=True)
                elif name == "ST":
                    pe.wait_ge(s_sel, b + 1)
                    settle(pe)
                    for t in range(T):
                        last = nc.tensor.transpose(bankF[0:E, P * t:P * t + P], sel[par][:, t, :], ident)
                else:
                    for t in range(T):
                        last = nc.tensor.matmul(bankF[:, C * t:C * t + C], selT[:, P * t:P * t + P], m["b2"][:], start=True, stop=True)
                last.then_inc(s_ff, 1)

            def hidden(n, e, par):
                for c in range(HC):
                    wait(pe, s_gelu, HC * (n - 1) + c + 1)
                    nc.tensor.matmul(bankH[c][:, 0:T * P], m["w1"][:, e, P * c:P * c + P], hTe[par][:], start=True, stop=True)\
                        .then_inc(s_hid, 1)

            def output(n, e):
                pe.wait_ge(s_gelu, HC * (n + 1))
                wait(pe, s_acc, n - 1)
                for t in range(T):
                    for c in range(HC):
                        last = nc.tensor.matmul(bankY[e % 2][:, C * t:C * t + C], hid[e % 2][:, c, P * t:P * t + P],
                                                m["w2"][:, HC * e + c, :], start=c == 0, stop=c == HC - 1)
                last.then_inc(s_y, 1)

            def slot(b, k, par):
                e, db = (k + 1) % E, (k + 1) // E
                if has(b + db, 0, B):
                    if db:
                        pe.wait_ge(s_fe, NF * (b + 1) + 1)
                    hidden(E * b + k + 1, e, (par + db) % 2)
                if has(b, 0, B):
                    output(E * b + k, k)
                if has(b, 0, B - 1):
                    for at, name in fronts:
                        if at == k:
                            front(b + 1, 1 - par, name)

            def prologue():
                pe.wait_ge(loads["ffn"], 16 * 5)
                for _, name in fronts:
                    front(0, 0, name)
                hidden(0, 0, 0)

            run(pe, E, slot, prologue, ahead=0, after=1)


RND = [1.5 * 2.0 ** 22, 1.5 * 2.0 ** 23, 1.5 * 2.0 ** 24]
TIE = 1.0 - 2.0 ** -24


class Quantiser:

    def __init__(self, nc, ctx, name, n):
        def sb(s, shape):
            return ctx.enter_context(nc.sbuf_tensor(f"{name}_{s}", shape, F32))
        self.nc, self.n = nc, n
        self.sc, self.rs = sb("sc", [P, n // 16]), sb("rs", [P, n // 16])
        self.v, self.a, self.z1, self.z2, self.z3 = (sb(s, [P, n]) for s in ("v", "a", "z1", "z2", "z3"))
        self.scaled, self.mag, self.parted, self.done = (ctx.enter_context(nc.semaphore(f"{name}_{s}"))
                                                         for s in ("scaled", "magnitudes", "parts", "quantised"))

    def scales(self, link, src, src3):
        v = self.nc.vector
        link(v.tensor_reduce(self.sc[:], src3, AX, ALU.max, apply_absolute_value=True))
        link(v.tensor_scalar(self.sc[:], self.sc[:], 1.0 / 6.0, 1e-12, ALU.mult, ALU.max))
        link(v.reciprocal(self.rs[:], self.sc[:]))
        v.tensor_tensor(self.v[:].rearrange("p (g k) -> p g k", k=16), src3,
                        self.rs[:].unsqueeze(2).to_broadcast([P, self.n // 16, 16]), ALU.mult).then_inc(self.scaled, 1)

    def magnitude(self, act, i):
        act.wait_ge(self.scaled, i + 1)
        wait(act, self.done, i)
        self.nc.scalar.activation(self.a[:], self.v[:], ACT.Abs, scale=TIE).then_inc(self.mag, 1)

    def parts(self, pool, i):
        pool.wait_ge(self.mag, i + 1)
        settle(pool)
        self.nc.gpsimd.tensor_scalar(self.z1[:], self.a[:], RND[0], RND[0] + 2.0, ALU.add, ALU.min)
        self.nc.gpsimd.tensor_scalar(self.z3[:], self.a[:], 4.0, RND[2], ALU.max, ALU.add).then_inc(self.parted, 1)

    def rebuild(self, dve, link, i, out):
        v = self.nc.vector
        dve.wait_ge(self.mag, i + 1)
        link(v.tensor_scalar(self.z2[:], self.a[:], 2.0, RND[1], ALU.max, ALU.add))
        link(v.tensor_scalar(self.z2[:], self.z2[:], RND[1] + 4.0, RND[1] + 2.0, ALU.min, ALU.subtract))
        dve.wait_ge(self.parted, i + 1)
        link(v.scalar_tensor_tensor(self.z2[:], self.z1[:], RND[0], self.z2[:], ALU.subtract, ALU.add))
        link(v.scalar_tensor_tensor(self.z2[:], self.z3[:], RND[2] + 4.0, self.z2[:], ALU.subtract, ALU.add))
        link(v.tensor_tensor(self.z2[:].rearrange("p (g k) -> p g k", k=16), self.z2[:].rearrange("p (g k) -> p g k", k=16),
                             self.sc[:].unsqueeze(2).to_broadcast([P, self.n // 16, 16]), ALU.mult))
        v.scalar_tensor_tensor(out.bitcast(I32), self.v[:].bitcast(I32), -2 ** 31, self.z2[:].bitcast(I32),
                               ALU.bitwise_and, ALU.bitwise_or).then_inc(self.done, 1)


def quant_ffn(nc, m, loads, out):
    with ExitStack() as ctx:
        def sb(name, shape, dt=F32):
            return ctx.enter_context(nc.sbuf_tensor(f"q_{name}", shape, dt))

        def sem(name):
            return ctx.enter_context(nc.semaphore(f"q_{name}"))

        stats, mv, veps, rstd = sb("stats", [P, T, 6]), sb("mv", [P, T, 2]), sb("veps", [P, T]), sb("rstd", [P, T])
        xn, xm, h = sb("xn", [P, T, C]), sb("xm", [P, T, C]), sb("h", [P, T, C])
        hq, hqT = sb("hq", [P, T * C]), sb("hqT", [P, T, P])
        sg, u = sb("sg", [P, T, FH]), sb("u", [P, T * FH])
        uq, uT = sb("uq", [P, T * FH]), sb("uT", [P, T, 3, P])
        yg = sb("yg", [P, T, C])
        wq, wdq = sb("wq", [P, 2 * 3 * C]), sb("wdq", [P, FH])
        wguT, wdT = sb("wguT", [P, 2, 3 * P]), sb("wdT", [P, 3, C])
        gu = ctx.enter_context(nc.psum_tensor("q_gu", [P, 4, 512], F32))
        bankX = ctx.enter_context(nc.psum_tensor("q_X", [P, 512], F32))
        bankU = [ctx.enter_context(nc.psum_tensor(f"q_U{t}", [P, 512], F32)) for t in range(T)]
        bankY = ctx.enter_context(nc.psum_tensor("q_Y", [P, 512], F32))
        guv = gu[:].rearrange("p (t a) k -> p t a k", a=2)
        qw1 = Quantiser(nc, ctx, "qw1", 2 * 3 * C)
        qw2 = Quantiser(nc, ctx, "qw2", FH)
        qx = Quantiser(nc, ctx, "qx", T * C)
        qu = Quantiser(nc, ctx, "qu", T * FH)
        x, con, rows = m["x"], m["con"], m["rows1"]
        ident = con[:, K_ID:K_ID + 128]
        (s_wT, s_wTe, s_xT, s_xTe, s_gu, s_sg, s_u, s_uT, s_uTe, s_y, s_yg, s_x, s_mv, s_rstd, s_xn, s_h, s_out, s_dch,
         s_pch) = [sem(n) for n in ["w_transposed", "w_ready", "x_transposed", "xT_ready", "gate_up_ready", "silu_ready", "u_ready",
                                    "u_transposed", "uT_ready", "y_ready", "yg_ready", "x_updated", "stats_ready", "rstd_ready",
                                    "xn_ready", "h_ready", "stored", "dve_chain", "pool_chain"]]
        block = ctx.enter_context(nc.Block())

        @block.sync
        def _(sp):
            for b in range(B):
                sp.wait_ge(s_x, b + 1)
                sp.dma_start(out[b].rearrange("(t p) f -> p t f", p=P), x[:, T * b:T * b + T, :]).then_inc(s_out, 16)
            sp.wait_ge(s_out, 16 * B)

        @block.gpsimd
        def _(pool):
            link = Chain(pool, s_pch)
            link.per_pair = 4

            def rstd_of(b):
                pool.wait_ge(s_mv, b + 1)
                settle(pool)
                link(nc.gpsimd.tensor_scalar_add(veps[:], mv[:, :, 1], 1e-5))
                nc.gpsimd.tensor_tensor(rstd[:], veps[:], m["mhalf"][:, 0:T], ALU.pow).then_inc(s_rstd, 1)

            def modulate(b):
                pool.wait_ge(s_xn, b + 1)
                wait(pool, s_h, b)
                link(nc.gpsimd.tensor_tensor(xm[:], xn[:], rows[:, b, 2 * C:3 * C].unsqueeze(1).to_broadcast([P, T, C]), ALU.mult))
                wait(pool, qx.scaled, b)
                nc.gpsimd.tensor_tensor(h[:], xm[:], rows[:, b, C:2 * C].unsqueeze(1).to_broadcast([P, T, C]), ALU.add)\
                    .then_inc(s_h, 1)

            def slot(b, k, par):
                if has(b, 0, B - 1):
                    modulate(b + 1)
                    qx.parts(pool, b + 1)
                if has(b, 0, B):
                    qu.parts(pool, b)
                if has(b, -1, B - 2):
                    rstd_of(b + 2)
                if has(b, 0, B):
                    pool.wait_ge(s_yg, b + 1)
                    xt = x[:, bass.ds(T * b, T), :]
                    nc.gpsimd.tensor_tensor(xt, xt, yg[:], ALU.add).then_inc(s_x, 1)

            def prologue():
                rstd_of(0)
                qw1.parts(pool, 0)
                qw2.parts(pool, 0)
                modulate(0)
                rstd_of(1)
                qx.parts(pool, 0)

            run(pool, 1, slot, prologue, [link], 0, 1)

        @block.vector
        def _(dve):
            link = Chain(dve, s_dch)
            link.per_pair = 2 * 17

            def stats_of(b):
                wait(dve, s_xn, b)
                for t in range(T):
                    last = nc.vector.bn_stats(stats[:, t, :], x[:, T * b + t, :])
                link(last)
                settle(dve)
                for t in range(T):
                    last = nc.vector.bn_aggr(mv[:, t, :], stats[:, t, :])
                last.then_inc(s_mv, 1)

            def normalise(b):
                dve.wait_ge(s_rstd, b + 1)
                wait(dve, s_h, b)
                for t in range(T):
                    last = nc.vector.tensor_scalar(xn[:, t, :], x[:, T * b + t, :], mv[:, t, 0:1], rstd[:, t:t + 1],
                                                   ALU.subtract, ALU.mult)
                last.then_inc(s_xn, 1)

            def scale_x(b):
                dve.wait_ge(s_h, b + 1)
                qx.scales(link, h, h[:].rearrange("p t (g k) -> p (t g) k", k=16))

            def rebuild_x(b):
                wait(dve, s_xT, b)
                qx.rebuild(dve, link, b, hq[:])

            def slot(b, k, par):
                if has(b, 0, B - 1):
                    normalise(b + 1)
                if has(b, 0, B):
                    dve.wait_ge(s_sg, b + 1)
                    nc.vector.tensor_tensor(u[:].rearrange("p (t f) -> p t f", t=T), guv[:, :, 1, 0:FH], sg[:], ALU.mult)\
                        .then_inc(s_u, 1)
                    dve.wait_ge(s_u, b + 1)
                    qu.scales(link, u, u[:].rearrange("p (g k) -> p g k", k=16))
                if has(b, 0, B - 1):
                    scale_x(b + 1)
                    rebuild_x(b + 1)
                if has(b, 0, B):
                    wait(dve, s_uT, b)
                    qu.rebuild(dve, link, b, uq[:])
                if has(b, -1, B - 2):
                    stats_of(b + 2)
                if has(b, 0, B):
                    dve.wait_ge(s_y, b + 1)
                    wait(dve, s_x, b)
                    nc.vector.tensor_tensor(yg[:], bankY[:, 0:T * C].rearrange("p (t c) -> p t c", t=T),
                                            rows[:, b, 3 * C:4 * C].unsqueeze(1).to_broadcast([P, T, C]), ALU.mult).then_inc(s_yg, 1)

            def prologue():
                stats_of(0)
                dve.wait_ge(loads["q"], 16 * 5)
                qw1.scales(link, None, m["wraw1"][:].rearrange("p a k (g j) -> p (a k g) j", j=16))
                qw2.scales(link, None, m["wraw2"][:].rearrange("p (g j) -> p g j", j=16))
                normalise(0)
                qw1.rebuild(dve, link, 0, wq[:])
                qw2.rebuild(dve, link, 0, wdq[:])
                stats_of(1)
                scale_x(0)
                rebuild_x(0)

            run(dve, 1, slot, prologue, [link], 0, 1)

        @block.scalar
        def _(act):
            def move_x(b):
                act.wait_ge(s_xT, b + 1)
                wait(act, s_gu, b)
                nc.scalar.copy(hqT[:], bankX[:, 0:T * P].rearrange("p (t q) -> p t q", t=T)).then_inc(s_xTe, 1)

            def silu(b):
                act.wait_ge(s_gu, b + 1)
                wait(act, s_u, b)
                nc.scalar.activation(sg[:], guv[:, :, 0, 0:FH], ACT.Silu).then_inc(s_sg, 1)

            def slot(b, k, par):
                if has(b, 0, B):
                    qu.magnitude(act, b)
                if has(b, 0, B - 1):
                    qx.magnitude(act, b + 1)
                    move_x(b + 1)
                    silu(b + 1)
                if has(b, 0, B):
                    act.wait_ge(s_uT, b + 1)
                    wait(act, s_y, b)
                    for t in range(T):
                        nc.scalar.copy(uT[:, t, 0:2, :], bankU[t][:, 0:2 * P].rearrange("p (c q) -> p c q", c=2))
                        last = nc.scalar.copy(uT[0:96, t, 2, :], bankU[t][0:96, 2 * P:3 * P])
                    last.then_inc(s_uTe, 1)

            def prologue():
                qw1.magnitude(act, 0)
                qw2.magnitude(act, 0)
                act.wait_ge(s_wT, 1)
                for a in range(2):
                    nc.scalar.copy(wguT[:, a, :], bankU[a][:, 0:3 * P])
                nc.scalar.copy(wdT[:, 0:2, :], bankX[:, 0:2 * P].rearrange("p (c q) -> p c q", c=2))
                nc.scalar.copy(wdT[0:96, 2, :], bankX[0:96, 2 * P:3 * P]).then_inc(s_wTe, 1)
                qx.magnitude(act, 0)
                move_x(0)
                silu(0)

            run(act, 1, slot, prologue, ahead=0, after=1)

        @block.tensor
        def _(pe):
            def gate_up(b):
                pe.wait_ge(qx.done, b + 1)
                wait(pe, s_xTe, b)
                for t in range(T):
                    last = nc.tensor.transpose(bankX[:, P * t:P * t + P], hq[:, C * t:C * t + C], ident)
                last.then_inc(s_xT, 1)
                pe.wait_ge(s_xTe, b + 1)
                wait(pe, s_u, b)
                for t in range(T):
                    for a in range(2):
                        last = nc.tensor.matmul(guv[:, t, a, 0:FH], hqT[:, t, :], wguT[:, a, 0:FH], start=True, stop=True)
                last.then_inc(s_gu, 1)

            def down(b):
                pe.wait_ge(qu.done, b + 1)
                wait(pe, s_uTe, b)
                for t in range(T):
                    for c, (at, w) in enumerate(FCH):
                        last = nc.tensor.transpose(bankU[t][0:w, P * c:P * c + P], uq[:, FH * t + at:FH * t + at + w], ident)
                last.then_inc(s_uT, 1)
                pe.wait_ge(s_uTe, b + 1)
                wait(pe, s_yg, b)
                for t in range(T):
                    for c, (at, w) in enumerate(FCH):
                        last = nc.tensor.matmul(bankY[:, C * t:C * t + C], uT[0:w, t, c, :], wdT[0:w, c, :], start=c == 0, stop=c == 2)
                last.then_inc(s_y, 1)

            def slot(b, k, par):
                if has(b, 0, B - 1):
                    gate_up(b + 1)
                if has(b, 0, B):
                    down(b)

            def prologue():
                pe.wait_ge(qw1.done, 1)
                pe.wait_ge(qw2.done, 1)
                for a in range(2):
                    for c in range(3):
                        nc.tensor.transpose(bankU[a][:, P * c:P * c + P], wq[:, 3 * C * a + C * c:3 * C * a + C * c + C], ident)
                for c, (at, w) in enumerate(FCH):
                    last = nc.tensor.transpose(bankX[0:w, P * c:P * c + P], wdq[:, at:at + w], ident)
                last.then_inc(s_wT, 1)
                pe.wait_ge(s_wTe, 1)
                gate_up(0)

            run(pe, 1, slot, prologue, ahead=0, after=1)


def constants(np):
    k = np.zeros((P, K_END), np.float32)
    row = np.arange(P)[:, None]
    k[:, K_ID:K_ID + 128] = np.eye(P)

    def window(W, t):
        kk = np.arange(2 * W)[None, :]
        i = row % W
        ok = (kk > i) & (kk <= i + W)
        if t == 0:
            ok &= (row // W > 0) | (kk >= W)
        return np.where(ok, 0.0, NEG)

    for t in range(T):
        k[:, K_LOC0 + 64 * t:K_LOC0 + 64 * t + 64] = window(32, t)
        k[:, K_LAT + 64 * t:K_LAT + 64 * t + 64] = np.where(np.arange(64)[None, :] <= (P * t + row) // 4, 0.0, NEG)
        k[:, K_LOC1 + 128 * t:K_LOC1 + 128 * t + 128] = window(64, t)
    q = np.arange(P)[None, :]
    s = np.float32(HD) ** -0.5
    k[:, K_Q0:K_Q0 + 128] = (row // 32 == q // 32) * s
    for g in range(2):
        k[:, K_Q1 + 128 * g:K_Q1 + 128 * g + 128] = ((row // 64 == q // 64) & (row % 64 // 32 == g)) * s
    k[:, K_S:K_S + 4] = row % 32 // 8 == np.arange(4)[None, :]
    k[:, K_GK:K_GK + 8] = (row // 8 == np.arange(8)[None, :]) * 0.25
    k[:, K_H:K_H + 16] = row // 8 == np.arange(16)[None, :]
    k[:, K_TRI:K_TRI + 64] = (np.arange(8)[None, :] < np.arange(8)[:, None]).reshape(1, 64)
    for b in range(B):
        k[b, K_SEL + 128 * b:K_SEL + 128 * b + 128] = 1.0
    return k


_INS = ["L0_attn_x", "L0_attn_wq", "L0_attn_wk", "L0_attn_wv", "L0_attn_wgq", "L0_attn_wgk", "L0_attn_wgv", "L0_attn_r_out_w",
        "L0_attn_gate_local_w", "L0_attn_gate_remote_w", "L0_attn_w_out", "L0_ffn_Wg", "L0_ffn_bg", "L0_ffn_W1", "L0_ffn_b1",
        "L0_ffn_W2", "L0_ffn_b2", "L0_c", "L0_wmod", "L1_attn_Wq", "L1_attn_Wk", "L1_attn_Wv", "L1_attn_Wo", "L1_ffn_w_gate",
        "L1_ffn_w_up", "L1_ffn_w_down", "L1_c", "L1_wmod"]


def kernel(**inputs):
    import numpy as np
    import concourse.bacc as bacc
    from concourse.bass_utils import run_bass_kernel_spmd
    nc = bacc.Bacc("TRN2", target_bir_lowering=False, num_devices=1)
    arrays, io = {}, {}
    for name in _INS:
        a = np.ascontiguousarray(inputs[name])
        arrays[f"in_{name}"] = a
        io[name] = nc.dram_tensor(f"in_{name}", a.shape, mybir.dt.from_np(a.dtype), kind="ExternalInput").ap()
    arrays["constants"] = constants(np)
    io["constants"] = nc.dram_tensor("constants", (P, K_END), F32, kind="ExternalInput").ap()
    out = nc.dram_tensor("out", (B, T * P, C), F32, kind="ExternalOutput").ap()
    build(nc, io, out)
    r = run_bass_kernel_spmd(nc, [arrays], core_ids=[0])
    return r.results[0]["out"]
```
